# Optimizing a Trainium2 kernel written in Bass

```python
import numpy as np
import jax
import jax.numpy as jnp

def _softmax(x, axis=-1):
    return jax.nn.softmax(x, axis=axis)

def _gelu(x):
    return jax.nn.gelu(x, approximate=True)

def _silu(x):
    return jax.nn.silu(x)

def _sigmoid(x):
    return jax.nn.sigmoid(x)

def _layernorm(x, axis=-1, eps=1e-05):
    m = jnp.mean(x, axis=axis, keepdims=True)
    v = jnp.var(x, axis=axis, keepdims=True)
    return (x - m) / jnp.sqrt(v + eps)

def _scatter_add(tgt, idx, src, axis=0):
    return tgt.at[idx].add(src)

def _segment_sum(src, seg, n):
    return jax.ops.segment_sum(src, seg, n)
kernel_name = 'mk_gnn_preln_d1_gnn_r8_b0e3b5'

def setup_inputs(seed: int=0):
    np.random.seed(seed)
    _w = jnp.asarray

    def _rec_inputs():
        import jax
        import jax.numpy as jnp
        _gk = jax.random.key(seed)
        x = -0.000202 + 1 * jax.random.normal(jax.random.fold_in(_gk, 1), (12500, 128), jnp.float32)
        _s = jax.random.randint(jax.random.fold_in(_gk, 2), (100000,), 0, 12500, jnp.int32)
        _d = jax.random.randint(jax.random.fold_in(_gk, 3), (100000,), 0, 12500, jnp.int32)
        _loop = jnp.arange(12500, dtype=jnp.int32)
        src = jnp.concatenate([_s, _d, _loop])
        dst = jnp.concatenate([_d, _s, _loop])
        _o = jnp.argsort(dst, stable=True)
        src = src[_o]
        dst = dst[_o]
        edge_attr_64 = 0.000189758 + 1.00013 * jax.random.normal(jax.random.fold_in(_gk, 12), (212500, 64), jnp.float32)
        return (x, src, dst, edge_attr_64)
    x, src, dst, edge_attr_64 = _rec_inputs()

    def _L0_gnn_setup():
        import jax, jax.numpy as jnp
        import numpy as np
        N = 6250
        E = 100000
        NF = 128
        EF = 64
        L = 256
        D1 = NF + EF + 1
        D2 = NF + L + 1
        NG = 64
        EPS = 1e-05

        def _bn(h, gamma, beta):
            mu = jnp.mean(h, axis=0, keepdims=True)
            var = jnp.var(h, axis=0, keepdims=True)
            return (h - mu) * jax.lax.rsqrt(var + EPS) * gamma + beta
        key = jax.random.key(seed)
        ks = jax.random.split(key, 12)
        x = jax.random.normal(ks[0], (N, NF), dtype=jnp.float32)
        edge_index = jax.random.randint(ks[1], (2, E), 0, N, dtype=jnp.int32)
        edge_attr = jax.random.normal(ks[2], (E, EF), dtype=jnp.float32)
        u = jax.random.normal(ks[3], (NG, 16), dtype=jnp.float32)
        batch = jnp.sort(jax.random.randint(ks[4], (N,), 0, NG, dtype=jnp.int32))
        s1 = 1.0 / np.sqrt(D1)
        s2 = 1.0 / np.sqrt(D2)
        W1 = jax.random.uniform(ks[5], (D1, L), minval=-s1, maxval=s1, dtype=jnp.float32)
        b1 = jax.random.uniform(ks[6], (L,), minval=-s1, maxval=s1, dtype=jnp.float32)
        W2 = jax.random.uniform(ks[7], (D2, D2), minval=-s2, maxval=s2, dtype=jnp.float32)
        b2 = jax.random.uniform(ks[8], (D2,), minval=-s2, maxval=s2, dtype=jnp.float32)
        W3 = jax.random.uniform(ks[9], (D2, NF), minval=-s2, maxval=s2, dtype=jnp.float32)
        b3 = jax.random.uniform(ks[10], (NF,), minval=-s2, maxval=s2, dtype=jnp.float32)
        g1 = jnp.ones((L,), jnp.float32)
        be1 = jnp.zeros((L,), jnp.float32)
        g2 = jnp.ones((D2,), jnp.float32)
        be2 = jnp.zeros((D2,), jnp.float32)
        return {'x': x, 'edge_index': edge_index, 'edge_attr': edge_attr, 'u': u, 'batch': batch, 'W1': W1, 'b1': b1, 'g1': g1, 'be1': be1, 'W2': W2, 'b2': b2, 'g2': g2, 'be2': be2, 'W3': W3, 'b3': b3}
    _L0_gnn_all = _L0_gnn_setup()
    _L0_gnn_in = {k: v for k, v in _L0_gnn_all.items() if k in ('u', 'W1', 'b1', 'g1', 'be1', 'W2', 'b2', 'g2', 'be2', 'W3', 'b3')}
    del _L0_gnn_all
    return {'x': x, 'src': src, 'dst': dst, 'edge_attr_64': edge_attr_64, 'L0_gnn_u': _L0_gnn_in['u'], 'L0_gnn_W1': _L0_gnn_in['W1'], 'L0_gnn_b1': _L0_gnn_in['b1'], 'L0_gnn_g1': _L0_gnn_in['g1'], 'L0_gnn_be1': _L0_gnn_in['be1'], 'L0_gnn_W2': _L0_gnn_in['W2'], 'L0_gnn_b2': _L0_gnn_in['b2'], 'L0_gnn_g2': _L0_gnn_in['g2'], 'L0_gnn_be2': _L0_gnn_in['be2'], 'L0_gnn_W3': _L0_gnn_in['W3'], 'L0_gnn_b3': _L0_gnn_in['b3']}

def reference(x, src, dst, edge_attr_64, L0_gnn_u, L0_gnn_W1, L0_gnn_b1, L0_gnn_g1, L0_gnn_be1, L0_gnn_W2, L0_gnn_b2, L0_gnn_g2, L0_gnn_be2, L0_gnn_W3, L0_gnn_b3):
    import jax
    import jax.numpy as jnp

    def _L0_gnn_ref(x, edge_index, edge_attr, u, batch, W1, b1, g1, be1, W2, b2, g2, be2, W3, b3):
        import jax, jax.numpy as jnp
        import numpy as np
        N = 6250
        E = 100000
        NF = 128
        EF = 64
        L = 256
        D1 = NF + EF + 1
        D2 = NF + L + 1
        NG = 64
        EPS = 1e-05

        def _bn(h, gamma, beta):
            mu = jnp.mean(h, axis=0, keepdims=True)
            var = jnp.var(h, axis=0, keepdims=True)
            return (h - mu) * jax.lax.rsqrt(var + EPS) * gamma + beta
        row, col = (edge_index[0], edge_index[1])
        bcol = batch.astype(x.dtype)[:, None]
        h = jnp.concatenate([x[row], bcol[row], edge_attr], axis=1)
        h = jax.nn.relu(_bn(h @ W1 + b1, g1, be1))
        ssum = jax.ops.segment_sum(h, col, num_segments=x.shape[0])
        cnt = jax.ops.segment_sum(jnp.ones((h.shape[0],), h.dtype), col, num_segments=x.shape[0])
        agg = ssum / jnp.maximum(cnt, 1.0)[:, None]
        h2 = jnp.concatenate([x, bcol, agg], axis=1)
        h2 = jax.nn.relu(_bn(h2 @ W2 + b2, g2, be2))
        return jax.nn.relu(h2 @ W3 + b3)
    edge_index = jnp.stack([src, dst])
    batch0 = jnp.zeros((12500,), jnp.int32)
    h = jnp.maximum(_layernorm(x, axis=-1), 0.0)
    x = x + _L0_gnn_ref(h, edge_index, edge_attr_64, L0_gnn_u, batch0, L0_gnn_W1, L0_gnn_b1, L0_gnn_g1, L0_gnn_be1, L0_gnn_W2, L0_gnn_b2, L0_gnn_g2, L0_gnn_be2, L0_gnn_W3, L0_gnn_b3)
    return x

_drawn_inputs = setup_inputs


def setup_inputs(seed=0):
    import zlib

    import numpy as np

    out = dict(_drawn_inputs(seed))
    spreads = {'L0_gnn_g1': (1.0, 0.6),
     'L0_gnn_be1': (0.0, 0.8),
     'L0_gnn_g2': (1.0, 0.2),
     'L0_gnn_be2': (0.0, 0.283)}
    factors = {'L0_gnn_b1': 8.0, 'L0_gnn_b2': 8.0}
    for name, (base, spread) in spreads.items():
        noise = np.random.default_rng([zlib.crc32(name.encode()), seed]).standard_normal(out[name].shape)
        drawn = base * np.exp(spread * noise) if base else spread * noise
        out[name] = jnp.asarray(drawn.astype(out[name].dtype))
    for name, factor in factors.items():
        out[name] = (out[name] * factor).astype(out[name].dtype)
    return out
```

```python
from contextlib import ExitStack

import concourse.bass as bass
from concourse import mybir

F32, I32, U32, BF16 = mybir.dt.float32, mybir.dt.int32, mybir.dt.uint32, mybir.dt.bfloat16
ALU, ACT, AX = mybir.AluOpType, mybir.ActivationFunctionType, mybir.AxisListType

P = 128
EPS = 1e-5
WIN = 128
GT = 4
GE = GT * P
EA_GROUPS = 4
EA_SLOTS = 3
M_SLOTS = 4
SMALLEST = 1e-20
ZERO_COLS = 1024


def ceil_div(a, b):
    return -(-a // b)


def build(nc, x, src_main, src_tail, dst_main, dst_tail, dst, eaT, W1, b1, g1, be1, W2, b2, g2, be2, W3, b3, out):
    N, NF = x.shape
    EF, E = eaT.shape
    L = W1.shape[1]
    D2 = W2.shape[0]
    assert NF == P and L == 2 * P and D2 == NF + L + 1
    KC = D2 // P
    GF = E // GE
    TAIL = E - GF * GE
    assert 0 < TAIL <= P and src_main.shape[1] == GF * GT
    NG = GF + 1
    TCOLS = GF * GT + 1
    BN_ = 4 * P
    EW = max(TCOLS, 8 * BN_ // 3 + 1)
    NH = ceil_div(N, P)
    NPAD = max(N + WIN, NH * P, 9600)
    NB = ceil_div(N, BN_)
    XC = 5
    NXC = ceil_div(NB, XC)
    GC = ceil_div(NG, P)
    EAU = ceil_div(NG, EA_GROUPS)
    assert NH <= P

    def block_nodes(b):
        return min(BN_, N - b * BN_)

    def tiles_of(b):
        return [(t, b * BN_ + t * P, min(P, N - b * BN_ - t * P)) for t in range(ceil_div(block_nodes(b), P))]

    def tiles(g):
        return GT if g < GF else 1

    def rows(g):
        return P if g < GF else TAIL

    P1_d = nc.dram_tensor("P1_d", (N, L), F32, kind="Internal").ap()
    hT_d = nc.dram_tensor("hT_d", (P, N), F32, kind="Internal").ap()
    m_d = nc.dram_tensor("m_d", (NG, P, GT * L), F32, kind="Internal").ap()
    range_d = nc.dram_tensor("range_d", (2 * GC, P), F32, kind="Internal").ap()
    cnt_d = nc.dram_tensor("cnt_d", (2, NH, P), F32, kind="Internal").ap()
    odd_d = nc.dram_tensor("odd_d", (1, N), F32, kind="Internal").ap()

    with ExitStack() as ctx:
        def sb(name, shape, dt=F32):
            return ctx.enter_context(nc.sbuf_tensor(name, shape, dt))

        def sem(name):
            return ctx.enter_context(nc.semaphore(name))

        sums = sb("sums", [P, 2, NPAD])
        area = sb("area", [P, max(N, 12288)])
        flat = sums[:, :, :].rearrange("p a n -> p (a n)")
        x_all = flat[:, 0:NB * BN_].rearrange("p (t f) -> p t f", f=NF)
        taken = [NB * BN_]

        def early(cols, parts=P):
            a = taken[0]
            taken[0] += cols
            assert taken[0] <= 2 * NPAD
            return flat[0:parts, a:a + cols]

        grp = early(GC * GE)
        grp_f = grp[:, 0:GC * GE].rearrange("p (c e) -> p c e", c=GC)
        grp_i = grp[:, 0:GC * GE].bitcast(I32).rearrange("p (c e) -> p c e", c=GC)
        h_row = [area[:, 512 * i:512 * i + 512].rearrange("p (t f) -> p t f", t=4) for i in range(2)]
        hT_s = [area[:, 1024 + 512 * i:1536 + 512 * i] for i in range(2)]
        p1_s = [area[:, 2048 + 1024 * i:3072 + 1024 * i].rearrange("p (t f) -> p t f", t=4) for i in range(2)]
        m_s = [area[:, 1024 * i:1024 * i + 1024] for i in range(M_SLOTS)]
        q_s = [area[:, 4096 + 1024 * i:5120 + 1024 * i] for i in range(2)]
        ea_s = [area[0:EF, 6144 + 2048 * i:8192 + 2048 * i] for i in range(EA_SLOTS)]
        plane = [sums[:, 0, :], sums[:, 1, :], area[:, :]]
        hT_n = area

        edges = sb("edges", [P, 4 * EW])
        idx = edges[:, 0:TCOLS].bitcast(I32)
        dst_f = edges[:, EW:EW + TCOLS]
        dst_hi = edges[:, 2 * EW:2 * EW + TCOLS]
        dst_lo = edges[:, 3 * EW:3 * EW + TCOLS]
        dst_hi_i, dst_lo_i = dst_hi.bitcast(I32), dst_lo.bitcast(I32)
        at = 6144
        sel = area[:, at:at + 4 * GT * WIN].rearrange("p (s k w) -> p s k w", s=4, k=GT)
        at += 4 * GT * WIN
        dist = area[:, at:at + 2 * GT * WIN].rearrange("p (s k w) -> p s k w", s=2, k=GT)
        at += 2 * GT * WIN
        MEAN, EX2, VAR, SD, RS, A, C, INV, NEGT = range(9)
        bn_row = area[:, at:at + 9 * L].rearrange("p (s f) -> p s f", f=L)
        assert at + 9 * L <= 12288
        nodebuf = edges[:, EW:EW + 4 * BN_].rearrange("p (s n) -> p s n", s=4)
        odd_o = edges[0:1, EW + 4 * BN_:EW + 6 * BN_].rearrange("p (s n) -> p s n", s=2)
        odd_x = edges[0:2, EW + 6 * BN_:EW + 8 * BN_].rearrange("p (s n) -> p s n", s=2)

        ident = sb("ident", [P, P])
        iota = sb("iota", [P, P])
        iota_b = sb("iota_b", [P, P], BF16)
        ones = sb("ones", [P, P])
        eps = sb("eps", [P, 1])
        bcol = sb("bcol", [P, 1])
        W1a = sb("W1a", [P, L])
        W1c = sb("W1c", [EF, L])
        b1_bc = sb("b1_bc", [P, L])
        W1b_bc = early(L)
        sgn = early(L)
        g1_bc, be1_bc = sb("g1_bc", [P, L]), sb("be1_bc", [P, L])
        W2s = sb("W2s", [P, 3, D2])
        W3s = sb("W3s", [P, KC, NF])
        W3o = sb("W3o", [2, NF])
        g2c, be2c, b2c, W2bc = (sb(n, [P, KC + 1]) for n in ("g2c", "be2c", "b2c", "W2bc"))
        ln_st = early(24 * NB).rearrange("p (t s) -> p t s", s=6)
        ln_mv = early(8 * NB).rearrange("p (t s) -> p t s", s=2)
        ln_r = early(4 * NB)
        ln_b = early(4 * NB)
        rng = sb("rng", [P, 2 * GC])
        rngT = sb("rngT", [2 * GC, P])
        base_bc = early(GC * P)
        rng_row = early(2 * GC * P, 1)
        base_i = sb("base_i", [1, GC * P], I32)
        wide = sb("wide", [1, 1])
        wide_i = sb("wide_i", [1, 1], I32)
        hot_hi = sb("hot_hi", [P, 2, GT, P], BF16)
        hot_lo = sb("hot_lo", [P, 2, GT, P], BF16)
        m_pair = sb("m_pair", [P, 2, 2 * L])
        a_col = sb("a_col", [P, 2])
        negt_col = sb("negt_col", [P, 2])
        T = sb("T", [P, L])
        cnt_s = sb("cnt_s", [NH, 2, P])
        bn2_st = sb("bn2_st", [P, KC + 1, NB, 6])
        bn2_mv = sb("bn2_mv", [P, KC + 1, 2])
        bn2 = sb("bn2", [P, 4, KC + 1])
        fb_sel = q_s[1][:, 0:GT * P].rearrange("p (k w) -> p k w", k=GT)
        fb_hi, fb_lo, fb_eq = sb("fb_hi", [P, GT]), sb("fb_lo", [P, GT]), sb("fb_eq", [P, GT])
        fb_w, fb_t = sb("fb_w", [P, 1]), sb("fb_t", [P, 1])
        cnt_bc = [nodebuf[:, i, :] for i in range(2)]
        inv_bc = [nodebuf[:, 2 + i, :] for i in range(2)]
        x_n = [nodebuf[:, i, :].rearrange("p (t f) -> p t f", t=4) for i in range(2)]
        o_n = [nodebuf[:, 2 + i, :].rearrange("p (t f) -> p t f", t=4) for i in range(2)]

        psum = ctx.enter_context(nc.psum_tensor("psum", [P, 8, 512], F32))
        ps_m = [psum[:, 2 * i:2 * i + 2, :].rearrange("p a b -> p (a b)") for i in range(2)]
        ps_sum, ps_sq, ps_cnt, ps_col = psum[:, 4, :], psum[:, 6, :], psum[:, 5, :], psum[:, 7, :]
        ps_seg = [psum[:, i, 0:2 * WIN] for i in range(2)]

        s_const = sem("s_const")
        s_w = sem("s_w")
        s_wp = sem("s_wp")
        s_x = [sem(f"s_x{i}") for i in range(NXC)]
        s_ei = sem("s_ei")
        s_grp = sem("s_grp")
        s_ei0 = sem("s_ei0")
        s_v = sem("s_v")
        s_sgn = sem("s_sgn")
        s_lnmv = sem("s_lnmv")
        s_lnsd = sem("s_lnsd")
        s_lnr = sem("s_lnr")
        s_h = sem("s_h")
        s_hT = sem("s_hT")
        s_hTs = sem("s_hTs")
        s_p1m = sem("s_p1m")
        s_p1 = sem("s_p1")
        s_p1w = [sem(f"s_p1w{i}") for i in range(2)]
        s_rng, s_rngT, s_rngs, s_rngw, s_rngl = (sem(n) for n in ("s_rng", "s_rngT", "s_rngs", "s_rngw", "s_rngl"))
        s_flag = sem("s_flag")
        s_gat = [[sem(f"s_gat{i}_{k}") for k in range(GT)] for i in range(M_SLOTS)]
        s_ea = [sem(f"s_ea{i}") for i in range(EA_SLOTS)]
        s_eam = sem("s_eam")
        s_m = sem("s_m")
        s_q = sem("s_q")
        s_hot = sem("s_hot")
        s_cnt = sem("s_cnt")
        s_pm = sem("s_pm")
        s_pq = sem("s_pq")
        s_st = sem("s_st")
        s_mw = [sem(f"s_mw{i}") for i in range(M_SLOTS)]
        s_var = sem("s_var")
        s_sd = sem("s_sd")
        s_row = sem("s_row")
        s_col = sem("s_col")
        s_cnts = sem("s_cnts")
        s_cntw = sem("s_cntw")
        s_ml = [sem(f"s_ml{i}") for i in range(M_SLOTS)]
        s_r = sem("s_r")
        s_sel = sem("s_sel")
        s_dist = sem("s_dist")
        s_seg = sem("s_seg")
        s_add = sem("s_add")
        s_B = sem("s_B")
        fb_free, fb_ld, fb_m, fb_e, fb_s, fb_pe, fb_add, fb_wc = (
            sem(n) for n in ("fb_free", "fb_ld", "fb_m", "fb_e", "fb_s", "fb_pe", "fb_add", "fb_wc"))
        s_hTl = [sem(f"s_hTl{i}") for i in range(NXC)]
        s_cl = [sem(f"s_cl{i}") for i in range(2)]
        s_n0 = sem("s_n0")
        s_n1 = sem("s_n1")
        s_n1s = sem("s_n1s")
        s_ow = [sem(f"s_ow{i}") for i in range(2)]
        s_ol = [sem(f"s_ol{i}") for i in range(2)]
        s_bst = sem("s_bst")
        s_v2, s_sd2, s_c2 = sem("s_v2"), sem("s_sd2"), sem("s_c2")
        s_ones = sem("s_ones")
        s_r2 = sem("s_r2")
        s_n2 = sem("s_n2")
        s_xn = [sem(f"s_xn{i}") for i in range(2)]
        s_o = sem("s_o")
        s_out = [sem(f"s_out{i}") for i in range(2)]

        block = ctx.enter_context(nc.Block())

        def row_tiles_dma(eng, dram, sbuf, b, to_sbuf, done):
            n = block_nodes(b)
            full = n // P
            parts = []
            if full:
                parts.append((dram[b * BN_:b * BN_ + full * P, :].rearrange("(t p) f -> p t f", p=P), sbuf[:, 0:full, :]))
            if n % P:
                parts.append((dram[b * BN_ + full * P:b * BN_ + n, :], sbuf[0:n % P, full, :]))
            for d, s in parts:
                eng.dma_start(s if to_sbuf else d, d if to_sbuf else s).then_inc(done, 16)
            return len(parts)

        def row_parts(b):
            n = block_nodes(b)
            return (1 if n // P else 0) + (1 if n % P else 0)

        def slot_count(b, per):
            return 16 * sum(per(i) for i in range(b % 2, b + 1, 2))

        x_parts = [sum(row_parts(b) for b in range(c * XC, min(NB, c * XC + XC))) for c in range(NXC)]
        W_LOADS, COLUMN_LOADS = 12, 8

        @block.sync
        def _(sp):
            for c in range(NXC):
                for b in range(c * XC, min(NB, c * XC + XC)):
                    row_tiles_dma(sp, x, x_all[:, 4 * b:4 * b + 4, :], b, True, s_x[c])
                if c == 0:
                    loads = [(W1a[:, :], W1[0:NF, :]), (W1c[:, :], W1[NF + 1:, :]),
                             (b1_bc[:, :], b1.partition_broadcast(P)), (W1b_bc[:, :], W1[NF, :].partition_broadcast(P)),
                             (g1_bc[:, :], g1.partition_broadcast(P)), (be1_bc[:, :], be1.partition_broadcast(P)),
                             (W2s[:, 0, :], W2[0:NF, :]), (W2s[:, 1, :], W2[NF + 1:NF + 1 + P, :]),
                             (W2s[:, 2, :], W2[NF + 1 + P:, :]),
                             (W3s[:, :, :], W3[0:KC * P, :].rearrange("(c p) f -> p c f", p=P)),
                             (W3o[0:1, :], W3[KC * P:, :]), (W3o[1:2, :], b3.rearrange("(a f) -> a f", a=1))]
                    for d, s in loads:
                        sp.dma_start(d, s).then_inc(s_w, 16)
            sp.wait_ge(s_ei0, 3)
            sp.dma_start(idx[:, 0:TCOLS - 1], src_main).then_inc(s_ei, 16)
            sp.dma_start(idx[0:TAIL, TCOLS - 1:], src_tail).then_inc(s_ei, 16)
            sp.dma_start(dst_hi_i[:, 0:TCOLS - 1], dst_main).then_inc(s_ei, 16)
            sp.dma_start(dst_hi_i[0:TAIL, TCOLS - 1:], dst_tail).then_inc(s_ei, 16)
            for c in range(GC):
                n = min(P, GF - c * P)
                sp.dma_start(grp_i[0:n, c, :], dst[c * GE * P:(c * P + n) * GE].rearrange("(g e) -> g e", e=GE)).then_inc(s_grp, 16)
            sp.dma_start(grp_i[GF % P:GF % P + 1, GF // P, :], dst[E - GE:E].rearrange("(g e) -> g e", g=1)).then_inc(s_grp, 16)

            def load_ea(u):
                if u >= EA_SLOTS:
                    sp.wait_ge(s_eam, EA_GROUPS * (u - EA_SLOTS + 1))
                a = u * EA_GROUPS * GE
                n = min(EA_GROUPS * GE, E - a)
                sp.dma_start(ea_s[u % EA_SLOTS][:, 0:n], eaT[:, a:a + n]).then_inc(s_ea[u % EA_SLOTS], 16)
            for u in range(min(EA_SLOTS, EAU)):
                load_ea(u)
            for b in range(NB):
                n = block_nodes(b)
                sp.wait_ge(s_hTs, b + 1)
                sp.dma_start(hT_d[:, b * BN_:b * BN_ + n], hT_s[b % 2][:, 0:n]).then_inc(s_p1w[b % 2], 16)
                sp.wait_ge(s_p1, b + 1)
                row_tiles_dma(sp, P1_d, p1_s[b % 2], b, False, s_p1w[b % 2])
            sp.wait_ge(s_rngs, 1)
            sp.dma_start(range_d, rngT[:, :]).then_inc(s_rngw, 16)
            sp.wait_ge(s_rngw, 16)
            sp.dma_start(base_bc[:, :], range_d[0:GC, :].rearrange("c p -> (c p)").partition_broadcast(P)).then_inc(s_rngl, 16)
            sp.dma_start(rng_row[:, :], range_d.rearrange("(a c) p -> a (c p)", a=1)).then_inc(s_rngl, 16)
            for g in range(NG):
                u = g // EA_GROUPS + 1
                if g % EA_GROUPS == EA_GROUPS - 1 and u + EA_SLOTS - 1 < EAU:
                    load_ea(u + EA_SLOTS - 1)
                sp.wait_ge(s_m, g + 1)
                r, w = rows(g), tiles(g) * L
                sp.dma_start(m_d[g, 0:r, 0:w], m_s[g % M_SLOTS][0:r, 0:w]).then_inc(s_mw[g % M_SLOTS], 16)
            sp.wait_ge(s_cnts, 1)
            sp.dma_start(cnt_d.rearrange("a h p -> h a p"), cnt_s[:, :, :]).then_inc(s_cntw, 16)
            for s in range(M_SLOTS):
                sp.wait_ge(s_mw[s], 16 * len(range(s, NG, M_SLOTS)))
            sp.wait_ge(s_st, NG)
            sp.wait_ge(s_flag, 1)
            flag = sp.alloc_register("wide_sp")
            sp.load(flag, wide_i[0:1, 0:1])
            with sp.If_eq(flag, 0):
                for g in range(NG):
                    if g >= M_SLOTS:
                        sp.wait_ge(s_seg, g - M_SLOTS + 1)
                    r, w = rows(g), tiles(g) * L
                    sp.dma_start(m_s[g % M_SLOTS][0:r, 0:w], m_d[g, 0:r, 0:w]).then_inc(s_ml[g % M_SLOTS], 16)
            with sp.Else():
                with sp.Fori(0, GF) as g:
                    sp.wait_ge(fb_free, g + 1)
                    sp.dma_start(m_s[0], m_d[bass.ds(g, 1), :, :].rearrange("g p w -> p (g w)")).then_inc(fb_ld, 16)
                sp.wait_ge(fb_free, GF + 1)
                sp.dma_start(m_s[0][0:TAIL, 0:L], m_d[GF, 0:TAIL, 0:L]).then_inc(fb_ld, 16)

            sp.wait_ge(s_B, 1)
            for i in range(2):
                sp.wait_ge(s_p1w[i], slot_count(NB - 1 - (NB - 1 - i) % 2, lambda b: 1 + row_parts(b)))
            for c in range(NXC):
                a, z = c * XC * BN_, min(N, (c + 1) * XC * BN_)
                sp.dma_start(hT_n[:, a:z], hT_d[:, a:z]).then_inc(s_hTl[c], 16)
            sp.wait_ge(s_cntw, 16)
            flat_cnt = cnt_d.rearrange("a h p -> a (h p)")
            for b in range(NB + 1):
                if b < NB:
                    n = block_nodes(b)
                    if b >= 2:
                        sp.wait_ge(s_n0, b - 1)
                    for a, d in ((0, cnt_bc), (1, inv_bc)):
                        sp.dma_start(d[b % 2][:, 0:n], flat_cnt[a, b * BN_:b * BN_ + n].partition_broadcast(P)).then_inc(s_cl[b % 2], 16)
                if b >= 1:
                    n = block_nodes(b - 1)
                    sp.wait_ge(s_n1s, b)
                    sp.dma_start(odd_d[:, (b - 1) * BN_:(b - 1) * BN_ + n], odd_o[:, (b - 1) % 2, 0:n]).then_inc(s_ow[(b - 1) % 2], 16)
            for i in range(2):
                sp.wait_ge(s_ow[i], 16 * len(range(i, NB, 2)))
            sp.wait_ge(s_n0, NB)
            sp.wait_ge(s_bst, NB)
            for b in range(NB + 1):
                if b < NB:
                    n = block_nodes(b)
                    if b >= 2:
                        sp.wait_ge(s_o, b - 1)
                        sp.wait_ge(s_r2, b - 1)
                    row_tiles_dma(sp, x, x_n[b % 2], b, True, s_xn[b % 2])
                    sp.dma_start(odd_o[:, b % 2, 0:n], odd_d[:, b * BN_:b * BN_ + n]).then_inc(s_ol[b % 2], 16)
                if b >= 1:
                    sp.wait_ge(s_o, b)
                    row_tiles_dma(sp, out, o_n[(b - 1) % 2], b - 1, False, s_out[(b - 1) % 2])
            for i in range(2):
                sp.wait_ge(s_out[i], slot_count(NB - 1 - (NB - 1 - i) % 2, row_parts))

        @block.gpsimd
        def _(pool):
            pool.memset(idx[:, TCOLS - 1:], 0).then_inc(s_ei0, 1)
            pool.memset(dst_hi_i[:, TCOLS - 1:], 0).then_inc(s_ei0, 1)
            pool.memset(grp_i, 0).then_inc(s_ei0, 1)
            pool.memset(ident[:, :], 0.0).then_inc(s_const, 1)
            pool.iota(iota[:, :], pattern=[[1, P]], base=0, channel_multiplier=0,
                      allow_small_or_imprecise_dtypes=True).then_inc(s_const, 1)
            pool.iota(iota_b[:, :], pattern=[[1, P]], base=0, channel_multiplier=0,
                      allow_small_or_imprecise_dtypes=True).then_inc(s_const, 1)
            pool.memset(ones[:, :], 1.0).then_inc(s_const, 1)
            pool.memset(eps[:, :], EPS).then_inc(s_const, 1)
            pool.memset(bcol[:, :], 0.0).then_inc(s_const, 1)
            pool.wait_ge(s_const, 6)
            pool.affine_select(out=ident[:, :], in_=ident[:, :], compare_op=ALU.not_equal, fill=1.0, base=0,
                               pattern=[[-1, P]], channel_multiplier=1).then_inc(s_const, 1)
            with nc.allow_non_contiguous_dma(reason="a few hundred parameters, once"):
                for v, c in ((g2, g2c), (be2, be2c), (b2, b2c), (W2[NF, :], W2bc)):
                    pool.dma_start(c[:, 0:KC], v[0:KC * P].rearrange("(c p) -> p c", p=P)).then_inc(s_wp, 16)
                    pool.dma_start(c[0:1, KC:], v[KC * P:].rearrange("(c p) -> p c", p=1)).then_inc(s_wp, 16)
            pool.wait_ge(s_ei, 64)
            for i in range(2):
                pool.wait_ge(s_p1w[i], slot_count(NB - 1 - (NB - 1 - i) % 2, lambda b: 1 + row_parts(b)))
            for g in range(NG):
                s, r = g % M_SLOTS, rows(g)
                if g >= M_SLOTS:
                    pool.wait_ge(s_mw[s], 16 * (g // M_SLOTS))
                    pool.wait_ge(s_pm, g - M_SLOTS + 1)
                    pool.wait_ge(s_q, g - M_SLOTS + 1)
                for k in range(tiles(g)):
                    pool.indirect_dma_start(
                        out=m_s[s][0:r, k * L:(k + 1) * L], out_offset=None, in_=P1_d,
                        in_offset=bass.IndirectOffsetOnAxis(ap=idx[0:r, GT * g + k:GT * g + k + 1].bitcast(U32), axis=0),
                    ).then_inc(s_gat[s][k], 16)
            pool.wait_ge(s_B, 1)
            pool.memset(odd_x, 1.0).then_inc(s_ones, 1)

        @block.scalar
        def _(act):
            act.wait_ge(s_const, 7)

            def chunk_tiles(c):
                return 4 * XC * c, min(4 * NB, 4 * XC * (c + 1))

            def ln_sqrt(c):
                a, z = chunk_tiles(c)
                act.wait_ge(s_lnmv, c + 1)
                act.activation(ln_r[:, a:z], ln_mv[:, a:z, 1], ACT.Sqrt, bias=eps[:, 0:1]).then_inc(s_lnsd, 1)

            def h_rows(b):
                if b >= 2:
                    act.wait_ge(s_hT, b - 1)
                for t, a, r in tiles_of(b):
                    i = 4 * b + t
                    ins = act.activation(h_row[b % 2][0:r, t, :], x_all[0:r, i, :], ACT.Relu,
                                         bias=ln_b[0:r, i:i + 1], scale=ln_r[0:r, i:i + 1])
                ins.then_inc(s_h, 1)

            def hT_copy(b):
                n = block_nodes(b)
                act.wait_ge(s_hT, b + 1)
                if b >= 2:
                    act.wait_ge(s_p1w[b % 2], slot_count(b - 2, lambda i: 1 + row_parts(i)))
                    act.wait_ge(s_p1m, b - 1)
                act.activation(hT_s[b % 2][:, 0:n], psum[:, 6 + b % 2, 0:n], ACT.Copy).then_inc(s_hTs, 1)

            ln_sqrt(0)
            for b in range(NB):
                c = b // XC
                if b % XC == 0:
                    act.wait_ge(s_lnr, c + 1)
                h_rows(b)
                if b >= 1:
                    hT_copy(b - 1)
                if b % XC == 1 and c + 1 < NXC:
                    ln_sqrt(c + 1)
            hT_copy(NB - 1)
            for g in range(NG):
                r, w = rows(g), tiles(g) * L
                act.wait_ge(s_m, g + 1)
                if g >= 2:
                    act.wait_ge(s_st, g - 1)
                act.activation(q_s[g % 2][0:r, 0:w], m_s[g % M_SLOTS][0:r, 0:w], ACT.Square).then_inc(s_q, 1)
            act.wait_ge(s_var, 1)
            act.activation(bn_row[:, SD, :], bn_row[:, VAR, :], ACT.Sqrt, bias=eps[:, 0:1]).then_inc(s_sd, 1)
            flag = act.alloc_register("wide_act")
            act.wait_ge(s_flag, 1)
            act.load(flag, wide_i[0:1, 0:1])
            with act.If_eq(flag, 0):
                for g in range(NG):
                    r, nt = rows(g), tiles(g)
                    if g >= 2:
                        act.wait_ge(s_sel, g - 1)
                    for k in range(max(1, nt - 1)):
                        ins = act.activation(dist[0:r, g % 2, k, :], iota[0:r, 0:WIN], ACT.Abs,
                                             bias=dst_f[0:r, GT * g + k:GT * g + k + 1])
                    ins.then_inc(s_dist, 1)
                    act.wait_ge(s_dist, g + 1)
                    if g >= 4:
                        act.wait_ge(s_seg, g - 3)
                    na = max(1, nt - 1)
                    act.activation(sel[0:r, g % 4, 0:na, :], dist[0:r, g % 2, 0:na, :], ACT.Relu,
                                   bias=ones[0:r, 0:1], scale=-1.0).then_inc(s_sel, 1)
            with act.Else():
                pass
            for b in range(NB):
                n, c0 = block_nodes(b), b * BN_
                act.wait_ge(s_n1, b + 1)
                bank = 4 * (b % 2)
                for c in range(KC):
                    act.activation(plane[c][:, c0:c0 + n], psum[:, bank + c, 0:n], ACT.Identity, bias=b2c[:, c:c + 1])
                if b >= 2:
                    act.wait_ge(s_ow[b % 2], 16 * (b // 2))
                    act.wait_ge(s_bst, b - 1)
                act.activation(odd_o[:, b % 2, 0:n], psum[0:1, bank + KC, 0:n], ACT.Identity,
                               bias=b2c[0:1, KC:]).then_inc(s_n1s, 1)
            act.wait_ge(s_v2, 1)
            act.activation(bn2[:, 0, 0:KC], bn2_mv[:, 0:KC, 1], ACT.Sqrt, bias=eps[:, 0:1])
            act.activation(bn2[0:1, 0, KC:], bn2_mv[0:1, KC:, 1], ACT.Sqrt, bias=eps[0:1, 0:1]).then_inc(s_sd2, 1)
            act.wait_ge(s_c2, 1)
            act.wait_ge(s_ones, 1)
            for b in range(NB):
                n, c0 = block_nodes(b), b * BN_
                for c in range(KC):
                    act.activation(plane[c][:, c0:c0 + n], plane[c][:, c0:c0 + n], ACT.Relu,
                                   bias=bn2[:, 3, c:c + 1], scale=bn2[:, 2, c:c + 1])
                act.wait_ge(s_ol[b % 2], 16 * (b // 2 + 1))
                if b >= 2:
                    act.wait_ge(s_n2, b - 1)
                act.activation(odd_x[0:1, b % 2, 0:n], odd_o[:, b % 2, 0:n], ACT.Relu,
                               bias=bn2[0:1, 3, KC:], scale=bn2[0:1, 2, KC:]).then_inc(s_r2, 1)

        @block.vector
        def _(dve):
            steps = [0]

            def step(ins):
                steps[0] += 1
                ins.then_inc(s_v, 1)
                dve.wait_ge(s_v, steps[0])

            dve.wait_ge(s_const, 7)

            def ln_stats(c):
                lo, hi = c * XC, min(NB, c * XC + XC)
                dve.wait_ge(s_x[c], 16 * x_parts[c])
                tl = [(4 * b + t, r) for b in range(lo, hi) for t, _, r in tiles_of(b)]
                for i, r in tl:
                    ins = dve.bn_stats(ln_st[0:r, i, :], x_all[0:r, i, :])
                step(ins)
                for i, r in tl:
                    ins = dve.bn_aggr(ln_mv[0:r, i, :], ln_st[0:r, i, :])
                ins.then_inc(s_lnmv, 1)

            def ln_scale(c):
                a, z = 4 * XC * c, min(4 * NB, 4 * XC * (c + 1))
                dve.wait_ge(s_lnsd, c + 1)
                step(dve.reciprocal(ln_r[:, a:z], ln_r[:, a:z]))
                dve.scalar_tensor_tensor(ln_b[:, a:z], ln_mv[:, a:z, 0], -1.0, ln_r[:, a:z],
                                         ALU.mult, ALU.mult).then_inc(s_lnr, 1)

            dve.memset(ln_mv[:, :, :], 0.0)
            step(dve.memset(bn2_mv[:, :, :], 0.0))
            ln_stats(0)
            dve.wait_ge(s_w, 16 * W_LOADS)
            dve.wait_ge(s_wp, 16 * COLUMN_LOADS)
            step(dve.tensor_scalar(sgn[:, :], g1_bc[:, :], 0.0, 2.0, ALU.is_ge, ALU.mult))
            step(dve.tensor_scalar(sgn[:, :], sgn[:, :], -1.0, None, ALU.add))
            dve.tensor_tensor(g1_bc[:, :], g1_bc[:, :], sgn[:, :], ALU.mult)
            step(dve.scalar_tensor_tensor(b1_bc[:, :], W1b_bc[:, :], bcol[:, 0:1], b1_bc[:, :], ALU.mult, ALU.add))
            dve.tensor_tensor(b1_bc[:, :], b1_bc[:, :], sgn[:, :], ALU.mult)
            dve.tensor_tensor(W1a[:, :], W1a[:, :], sgn[:, :], ALU.mult)
            step(dve.tensor_tensor(W1c[:, :], W1c[:, :], sgn[0:EF, :], ALU.mult))
            dve.scalar_tensor_tensor(b2c[:, 0:KC], W2bc[:, 0:KC], bcol[:, 0:1], b2c[:, 0:KC], ALU.mult, ALU.add)
            dve.scalar_tensor_tensor(b2c[0:1, KC:], W2bc[0:1, KC:], bcol[0:1, 0:1], b2c[0:1, KC:],
                                     ALU.mult, ALU.add).then_inc(s_sgn, 1)

            def table_rows(b):
                dve.wait_ge(s_p1m, b + 1)
                if b >= 2:
                    dve.wait_ge(s_p1w[b % 2], slot_count(b - 2, lambda i: 1 + row_parts(i)))
                for t, _, r in tiles_of(b):
                    if t % 2 == 0:
                        n2 = min(2, len(tiles_of(b)) - t)
                        if all(q[2] == P for q in tiles_of(b)[t:t + n2]):
                            parts = [(t, n2, P)]
                        else:
                            parts = [(q[0], 1, q[2]) for q in tiles_of(b)[t:t + n2]]
                        for t0, m, rr in parts:
                            ins = dve.tensor_tensor(
                                p1_s[b % 2][0:rr, t0:t0 + m, :],
                                ps_m[b % 2][0:rr, t0 * L:(t0 + m) * L].rearrange("p (t f) -> p t f", f=L),
                                b1_bc[0:rr, :].unsqueeze(1).to_broadcast([rr, m, L]), ALU.add)
                ins.then_inc(s_p1, 1)

            ln_scale(0)
            if NXC > 1:
                ln_stats(1)
            for c in range(NXC):
                for b in range(c * XC, min(NB, c * XC + XC)):
                    table_rows(b)
                    if b % XC == 1 and c + 1 < NXC:
                        ln_scale(c + 1)
                    if b % XC == 2 and c + 2 < NXC:
                        ln_stats(c + 2)
                if c == 0:
                    dve.wait_ge(s_ei, 64)
                    dve.tensor_copy(dst_f[:, :], dst_hi_i[:, :])
                    step(dve.tensor_scalar(dst_lo_i[:, :], dst_hi_i[:, :], P - 1, None, ALU.bitwise_and))
                    step(dve.tensor_scalar(dst_hi_i[:, :], dst_hi_i[:, :], P.bit_length() - 1, None,
                                           ALU.logical_shift_right))
                    dve.tensor_copy(dst_hi, dst_hi_i[:, :])
                    step(dve.tensor_copy(dst_lo, dst_lo_i[:, :]))
                    dve.wait_ge(s_grp, 16 * (GC + 1))
                    step(dve.tensor_copy(grp_f, grp_i))
                    step(dve.tensor_reduce(rng[:, 0:GC], grp_f, AX.X, ALU.min))
                    step(dve.tensor_reduce(rng[:, GC:], grp_f, AX.X, ALU.max))
                    dve.tensor_tensor(rng[:, GC:], rng[:, GC:], rng[:, 0:GC], ALU.subtract).then_inc(s_rng, 1)
            dve.wait_ge(s_rngT, 1)
            dve.tensor_copy(rngT[:, :], psum[0:2 * GC, 5, 0:P]).then_inc(s_rngs, 1)
            dve.wait_ge(s_rngl, 32)

            def one_hot(g):
                if g >= 2:
                    dve.wait_ge(s_cnt, g - 1)
                r = rows(g)
                for k in range(tiles(g)):
                    j = GT * g + k
                    dve.tensor_scalar(hot_hi[0:r, g % 2, k, 0:NH], iota_b[0:r, 0:NH], dst_hi[0:r, j:j + 1], None, ALU.is_equal)
                    ins = dve.tensor_scalar(hot_lo[0:r, g % 2, k, :], iota_b[0:r, :], dst_lo[0:r, j:j + 1], None, ALU.is_equal)
                ins.then_inc(s_hot, 1)

            one_hot(0)
            dve.tensor_copy(base_i[:, :], rng_row[:, 0:GC * P])
            step(dve.tensor_reduce(wide[:, :], rng_row[:, GC * P:], AX.X, ALU.max))
            step(dve.tensor_scalar(wide[:, :], wide[:, :], float(WIN), None, ALU.is_ge))
            dve.tensor_copy(wide_i[:, :], wide[:, :])
            dve.tensor_tensor(dst_f[:, TCOLS - 1:], base_bc[:, GF:GF + 1], dst_f[:, TCOLS - 1:], ALU.subtract)
            main = dst_f[:, 0:GF * GT].rearrange("p (g k) -> p g k", k=GT)
            dve.tensor_tensor(main, base_bc[:, 0:GF].unsqueeze(2).to_broadcast([P, GF, GT]), main,
                              ALU.subtract).then_inc(s_flag, 1)
            zero_at = 0
            dve.wait_ge(s_h, NB)
            H2 = 2 * L
            for g in range(NG):
                s, r, w = g % M_SLOTS, rows(g), tiles(g) * L
                if zero_at < 2 * NPAD:
                    z = min(2 * NPAD, zero_at + ZERO_COLS)
                    dve.memset(flat[:, zero_at:z], 0.0)
                    zero_at = z
                if g >= 1:
                    dve.wait_ge(s_q, g)
                    q = q_s[(g - 1) % 2]
                    dve.tensor_tensor(q[:, 0:H2], q[:, 0:H2], q[:, H2:2 * H2], ALU.add).then_inc(s_pq, 1)
                for k in range(tiles(g)):
                    dve.wait_ge(s_gat[s][k], 16 * (g // M_SLOTS + 1))
                dve.wait_ge(s_eam, g + 1)
                dve.tensor_tensor(m_s[s][0:r, 0:w], ps_m[g % 2][0:r, 0:w], m_s[s][0:r, 0:w], ALU.add).then_inc(s_m, 1)
                if g + 1 < NG:
                    one_hot(g + 1)
                if g < GF:
                    dve.wait_ge(s_m, g + 1)
                    if g >= 2:
                        dve.wait_ge(s_st, g - 1)
                    dve.tensor_tensor(m_pair[:, g % 2, :], m_s[s][:, 0:H2], m_s[s][:, H2:2 * H2], ALU.add).then_inc(s_pm, 1)
            while zero_at < 2 * NPAD:
                z = min(2 * NPAD, zero_at + ZERO_COLS)
                step(dve.memset(flat[:, zero_at:z], 0.0))
                zero_at = z
            dve.wait_ge(s_st, NG)
            for ps, row in ((ps_sum, MEAN), (ps_sq, EX2)):
                step(dve.tensor_scalar(bn_row[:, row, :], ps[:, 0:L], 1.0 / E, None, ALU.mult))
                step(dve.scalar_tensor_tensor(bn_row[:, row, :], ps[:, L:2 * L], 1.0 / E, bn_row[:, row, :],
                                              ALU.mult, ALU.add))
            step(dve.tensor_tensor(bn_row[:, VAR, :], bn_row[:, MEAN, :], bn_row[:, MEAN, :], ALU.mult))
            step(dve.tensor_tensor(bn_row[:, VAR, :], bn_row[:, EX2, :], bn_row[:, VAR, :], ALU.subtract))
            dve.tensor_scalar(bn_row[:, VAR, :], bn_row[:, VAR, :], 0.0, None, ALU.max).then_inc(s_var, 1)
            dve.wait_ge(s_sd, 1)
            step(dve.reciprocal(bn_row[:, RS, :], bn_row[:, SD, :]))
            step(dve.tensor_tensor(bn_row[:, A, :], g1_bc[:, :], bn_row[:, RS, :], ALU.mult))
            step(dve.tensor_tensor(bn_row[:, C, :], bn_row[:, A, :], bn_row[:, MEAN, :], ALU.mult))
            step(dve.tensor_tensor(bn_row[:, C, :], be1_bc[:, :], bn_row[:, C, :], ALU.subtract))
            step(dve.tensor_scalar(bn_row[:, A, :], bn_row[:, A, :], SMALLEST, None, ALU.max))
            step(dve.reciprocal(bn_row[:, INV, :], bn_row[:, A, :]))
            dve.tensor_tensor(bn_row[:, NEGT, :], bn_row[:, C, :], bn_row[:, INV, :], ALU.mult).then_inc(s_row, 1)
            dve.wait_ge(s_row, 1)
            step(dve.tensor_scalar(T[:, :], bn_row[:, NEGT, :], -1.0, None, ALU.mult))
            dve.wait_ge(s_cnt, NG)
            step(dve.tensor_copy(cnt_s[:, 0, :], ps_cnt[0:NH, 0:P]))
            step(dve.tensor_scalar(cnt_s[:, 1, :], cnt_s[:, 0, :], 1.0, None, ALU.max))
            dve.reciprocal(cnt_s[:, 1, :], cnt_s[:, 1, :]).then_inc(s_cnts, 1)

            flag = dve.alloc_register("wide_dve")
            dve.load(flag, wide_i[0:1, 0:1])

            def clip(r, nt, slot):
                v = m_s[slot][0:r, 0:nt * L].rearrange("p (k f) -> p k f", f=L)
                return dve.tensor_tensor(v, v, T[0:r, :].unsqueeze(1).to_broadcast([r, nt, L]), ALU.max)

            with dve.If_eq(flag, 0):
                def add_window(g):
                    at = dve.value_load(base_i[0:1, g:g + 1], min_val=0, max_val=N - 1)
                    dve.wait_ge(s_seg, g + 1)
                    if g:
                        dve.wait_ge(s_add, g)
                    win = sums[:, :, bass.ds(at, WIN)]
                    dve.tensor_tensor(win, win, ps_seg[g % 2].rearrange("p (h w) -> p h w", h=2),
                                      ALU.add).then_inc(s_add, 1)
                for g in range(NG):
                    s = g % M_SLOTS
                    if g < GF:
                        if g >= 4:
                            dve.wait_ge(s_seg, g - 3)
                        dve.tensor_scalar(sel[:, g % 4, GT - 1, :], iota[:, :], dst_f[:, GT * g + GT - 1:GT * g + GT],
                                          0.0, ALU.add, ALU.is_equal)
                    dve.wait_ge(s_ml[s], 16 * (g // M_SLOTS + 1))
                    clip(rows(g), tiles(g), s).then_inc(s_r, 1)
                    if g >= 1:
                        add_window(g - 1)
                add_window(NG - 1)
                dve.wait_ge(s_add, NG)
                dve.memset(fb_t[:, :], 0.0).then_inc(s_B, 1)
            with dve.Else():
                def group(g, r, nt, first):
                    dve.wait_ge(fb_ld, (g + 1) * 16)
                    clip(r, nt, 0).then_inc(fb_m, 1)
                    if first is None:
                        dve.tensor_copy(fb_hi[0:r, 0:nt], dst_hi[0:r, TCOLS - 1:]).then_inc(fb_m, 1)
                        dve.tensor_copy(fb_lo[0:r, 0:nt], dst_lo[0:r, TCOLS - 1:]).then_inc(fb_m, 1)
                    else:
                        dve.tensor_copy(fb_hi[:, :], dst_hi[:, bass.ds(g * GT, GT)]).then_inc(fb_m, 1)
                        dve.tensor_copy(fb_lo[:, :], dst_lo[:, bass.ds(g * GT, GT)]).then_inc(fb_m, 1)
                    dve.memset(fb_w[:, :], 0.0).then_inc(fb_m, 1)
                    dve.wait_ge(fb_m, (g + 1) * 4)
                    dve.tensor_copy(fb_t[:, :], fb_w[:, :])
                    with dve.Fori(0, NH) as w:
                        i = g * NH + w
                        dve.tensor_scalar(fb_eq[0:r, 0:nt], fb_hi[0:r, 0:nt], fb_w[0:r, 0:1], None,
                                          ALU.is_equal).then_inc(fb_e, 1)
                        dve.wait_ge(fb_e, i + 1)
                        for k in range(nt):
                            ins = dve.tensor_scalar(fb_sel[0:r, k, :], iota[0:r, :], fb_lo[0:r, k:k + 1],
                                                    fb_eq[0:r, k:k + 1], ALU.is_equal, ALU.mult)
                        ins.then_inc(fb_s, 1)
                        dve.tensor_scalar(fb_w[:, :], fb_w[:, :], 1.0, None, ALU.add).then_inc(fb_wc, 1)
                        dve.wait_ge(fb_wc, i + 1)
                        dve.wait_ge(fb_pe, i + 1)
                        win = sums[:, :, bass.ds(w * P, P)]
                        dve.tensor_tensor(win, win, psum[:, 0, 0:2 * P].rearrange("p (h w) -> p h w", h=2),
                                          ALU.add).then_inc(fb_add, 1)
                        dve.wait_ge(fb_add, i + 1)
                    dve.memset(fb_t[:, :], 0.0).then_inc(fb_free, 1)
                dve.memset(fb_t[:, :], 0.0).then_inc(fb_free, 1)
                with dve.Fori(0, GF) as g:
                    group(g, P, GT, 0)
                group(GF, TAIL, 1, None)
                dve.wait_ge(fb_free, GF + 2)
                dve.memset(fb_t[:, :], 0.0).then_inc(s_B, 1)

            dve.wait_ge(s_col, 1)
            cols = ps_col.rearrange("p (v f) -> p v f", f=P)[:, :, 0]
            dve.tensor_copy(a_col[:, :], cols[:, 0:2])
            step(dve.tensor_copy(negt_col[:, :], cols[:, 2:4]))
            for h in range(2):
                step(dve.tensor_scalar(W2s[:, 1 + h, :], W2s[:, 1 + h, :], a_col[:, h:h + 1], None, ALU.mult))

            def agg(b):
                n, c0 = block_nodes(b), b * BN_
                dve.wait_ge(s_cl[b % 2], 32 * (b // 2 + 1))
                for h in range(2):
                    v = sums[:, h, c0:c0 + n]
                    ins = dve.scalar_tensor_tensor(v, cnt_bc[b % 2][:, 0:n], negt_col[:, h:h + 1], v, ALU.mult, ALU.add)
                step(ins)
                v = sums[:, :, c0:c0 + n]
                dve.tensor_tensor(v, v, inv_bc[b % 2][:, 0:n].unsqueeze(1).to_broadcast([P, 2, n]),
                                  ALU.mult).then_inc(s_n0, 1)

            def pre_stats(b):
                n, c0 = block_nodes(b), b * BN_
                dve.wait_ge(s_n1s, b + 1)
                for c in range(KC):
                    dve.bn_stats(bn2_st[:, c, b, :], plane[c][:, c0:c0 + n])
                dve.bn_stats(bn2_st[0:1, KC, b, :], odd_o[:, b % 2, 0:n]).then_inc(s_bst, 1)

            dve.wait_ge(s_B, 1)
            for b in range(NB):
                agg(b)
                if b >= 1:
                    pre_stats(b - 1)
            pre_stats(NB - 1)
            dve.wait_ge(s_bst, NB)
            for c in range(KC):
                dve.bn_aggr(bn2_mv[:, c, :], bn2_st[:, c, :, :].rearrange("p b s -> p (b s)"))
            dve.bn_aggr(bn2_mv[0:1, KC, :], bn2_st[0:1, KC, :, :].rearrange("p b s -> p (b s)")).then_inc(s_v2, 1)
            dve.wait_ge(s_sd2, 1)
            for p, a, z in ((P, 0, KC), (1, KC, KC + 1)):
                step(dve.reciprocal(bn2[0:p, 1, a:z], bn2[0:p, 0, a:z]))
                step(dve.tensor_tensor(bn2[0:p, 2, a:z], g2c[0:p, a:z], bn2[0:p, 1, a:z], ALU.mult))
                step(dve.tensor_tensor(bn2[0:p, 3, a:z], bn2[0:p, 2, a:z], bn2_mv[0:p, a:z, 0], ALU.mult))
                ins = dve.tensor_tensor(bn2[0:p, 3, a:z], be2c[0:p, a:z], bn2[0:p, 3, a:z], ALU.subtract)
                if p == P:
                    step(ins)
                else:
                    ins.then_inc(s_c2, 1)
            for b in range(NB):
                dve.wait_ge(s_n2, b + 1)
                dve.wait_ge(s_xn[b % 2], slot_count(b, row_parts))
                if b >= 2:
                    dve.wait_ge(s_out[b % 2], slot_count(b - 2, row_parts))
                tl = tiles_of(b)
                full = sum(1 for q in tl if q[2] == P)
                parts = ([(0, full, P)] if full else []) + [(q[0], 1, q[2]) for q in tl if q[2] < P]
                for t0, m, r in parts:
                    ins = dve.scalar_tensor_tensor(
                        o_n[b % 2][0:r, t0:t0 + m, :],
                        psum[0:r, b % 2, t0 * P:(t0 + m) * P].rearrange("p (t f) -> p t f", f=NF), 0.0,
                        x_n[b % 2][0:r, t0:t0 + m, :], ALU.max, ALU.add)
                ins.then_inc(s_o, 1)

        @block.tensor
        def _(pe):
            pe.wait_ge(s_const, 7)
            pe.wait_ge(s_sgn, 1)

            def turn(b):
                pe.wait_ge(s_h, b + 1)
                if b >= 2:
                    pe.wait_ge(s_hTs, b - 1)
                for t, _, r in tiles_of(b):
                    ins = pe.transpose(psum[:, 6 + b % 2, t * P:t * P + r], h_row[b % 2][0:r, t, :], ident[0:r, 0:r])
                ins.then_inc(s_hT, 1)

            def table(b):
                pe.wait_ge(s_hTs, b + 1)
                if b >= 2:
                    pe.wait_ge(s_p1, b - 1)
                for t, _, r in tiles_of(b):
                    ins = pe.matmul(ps_m[b % 2][0:r, t * L:(t + 1) * L], hT_s[b % 2][:, t * P:t * P + r], W1a[:, :],
                                    start=True, stop=True)
                ins.then_inc(s_p1m, 1)

            for b in range(NB):
                turn(b)
                if b >= 1:
                    table(b - 1)
            table(NB - 1)
            pe.wait_ge(s_rng, 1)
            pe.transpose(psum[0:2 * GC, 5, 0:P], rng[:, :], ident[:, :]).then_inc(s_rngT, 1)
            pe.wait_ge(s_p1, NB)
            pe.wait_ge(s_rngs, 1)

            def stats(g):
                if g < GF:
                    pe.wait_ge(s_pm, g + 1)
                    pe.wait_ge(s_pq, g + 1)
                    r, w, m = P, 2 * L, m_pair[:, g % 2, :]
                else:
                    pe.wait_ge(s_q, g + 1)
                    r, w, m = TAIL, L, m_s[g % M_SLOTS]
                for ps, v in ((ps_sum, m), (ps_sq, q_s[g % 2])):
                    ins = pe.matmul(ps[:, 0:w], ones[0:r, :], v[0:r, 0:w], start=(g == 0), stop=(g == NG - 1),
                                    skip_group_check=True)
                ins.then_inc(s_st, 1)

            for g in range(NG):
                u, r = g // EA_GROUPS, rows(g)
                if g % EA_GROUPS == 0:
                    pe.wait_ge(s_ea[u % EA_SLOTS], 16 * (u // EA_SLOTS + 1))
                if g >= 2:
                    pe.wait_ge(s_m, g - 1)
                for k in range(tiles(g)):
                    a = (g % EA_GROUPS) * GE + k * P
                    ins = pe.matmul(ps_m[g % 2][0:r, k * L:(k + 1) * L], ea_s[u % EA_SLOTS][:, a:a + r], W1c[:, :],
                                    start=True, stop=True)
                ins.then_inc(s_eam, 1)
                pe.wait_ge(s_hot, g + 1)
                for k in range(tiles(g)):
                    ins = pe.matmul(ps_cnt[0:NH, 0:P], hot_hi[0:r, g % 2, k, 0:NH], hot_lo[0:r, g % 2, k, :],
                                    start=(g == 0 and k == 0), stop=(g == NG - 1), skip_group_check=True)
                ins.then_inc(s_cnt, 1)
                if g >= 1:
                    stats(g - 1)
            stats(NG - 1)
            pe.wait_ge(s_row, 1)
            for i, (v, h) in enumerate(((A, 0), (A, 1), (NEGT, 0), (NEGT, 1))):
                ins = pe.transpose(ps_col[:, i * P:(i + 1) * P], bn_row[:, v, h * P:(h + 1) * P], ident[:, :])
            ins.then_inc(s_col, 1)

            def window(nt, r, slot, sel_k, width, bank_ap, done):
                for k in range(nt):
                    for h in range(2):
                        ins = pe.matmul(bank_ap[:, h * width:(h + 1) * width],
                                        m_s[slot][0:r, k * L + h * P:k * L + (h + 1) * P], sel_k(k)[0:r, :],
                                        start=(k == 0 and h == 0), stop=(k == nt - 1), skip_group_check=True)
                ins.then_inc(done, 1)

            flag = pe.alloc_register("wide_pe")
            pe.wait_ge(s_flag, 1)
            pe.load(flag, wide_i[0:1, 0:1])
            with pe.If_eq(flag, 0):
                for g in range(NG):
                    pe.wait_ge(s_r, g + 1)
                    pe.wait_ge(s_sel, g + 1)
                    if g >= 2:
                        pe.wait_ge(s_add, g - 1)
                    window(tiles(g), rows(g), g % M_SLOTS, lambda k, g=g: sel[:, g % 4, k, :], WIN, ps_seg[g % 2], s_seg)
            with pe.Else():
                with pe.Fori(0, GF) as g:
                    with pe.Fori(0, NH) as w:
                        pe.wait_ge(fb_s, g * NH + w + 1)
                        window(GT, P, 0, lambda k: fb_sel[:, k, :], P, psum[:, 0, :], fb_pe)
                with pe.Fori(0, NH) as w:
                    pe.wait_ge(fb_s, w + (GF * NH + 1))
                    window(1, TAIL, 0, lambda k: fb_sel[:, k, :], P, psum[:, 0, :], fb_pe)

            for b in range(NB):
                n, c0 = block_nodes(b), b * BN_
                if b % XC == 0:
                    pe.wait_ge(s_hTl[b // XC], 16)
                pe.wait_ge(s_n0, b + 1)
                if b >= 2:
                    pe.wait_ge(s_n1s, b - 1)
                for c in range(KC + 1):
                    mo = P if c < KC else 1
                    for k, operand in enumerate((hT_n, plane[0], plane[1])):
                        ins = pe.matmul(psum[0:mo, 4 * (b % 2) + c, 0:n], W2s[:, k, c * P:c * P + mo],
                                        operand[:, c0:c0 + n], start=(k == 0), stop=(k == 2))
                ins.then_inc(s_n1, 1)
            pe.wait_ge(s_n1s, NB)
            for b in range(NB):
                pe.wait_ge(s_r2, b + 1)
                if b >= 2:
                    pe.wait_ge(s_o, b - 1)
                for t, a, r in tiles_of(b):
                    o = psum[0:r, b % 2, t * P:(t + 1) * P]
                    for c in range(KC):
                        pe.matmul(o, plane[c][:, a:a + r], W3s[:, c, :], start=(c == 0), stop=False)
                    ins = pe.matmul(o, odd_x[0:2, b % 2, t * P:t * P + r], W3o[:, :], start=False, stop=True)
                ins.then_inc(s_n2, 1)


def kernel(x, src, dst, edge_attr_64, L0_gnn_u, L0_gnn_W1, L0_gnn_b1, L0_gnn_g1, L0_gnn_be1, L0_gnn_W2,
           L0_gnn_b2, L0_gnn_g2, L0_gnn_be2, L0_gnn_W3, L0_gnn_b3):
    import numpy as np
    import concourse.bacc as bacc
    from concourse.bass_utils import run_bass_kernel_spmd

    src, dst = np.asarray(src), np.asarray(dst)
    full = src.shape[0] // GE * GE

    def columns(v):
        return np.ascontiguousarray(v[:full].reshape(-1, P).T), np.ascontiguousarray(v[full:].reshape(-1, 1))

    src_main, src_tail = columns(src)
    dst_main, dst_tail = columns(dst)
    arrays = {
        "x": x, "src_main": src_main, "src_tail": src_tail, "dst_main": dst_main, "dst_tail": dst_tail, "dst": dst,
        "eaT": np.ascontiguousarray(np.asarray(edge_attr_64).T),
        "W1": L0_gnn_W1, "b1": L0_gnn_b1, "g1": L0_gnn_g1, "be1": L0_gnn_be1,
        "W2": L0_gnn_W2, "b2": L0_gnn_b2, "g2": L0_gnn_g2, "be2": L0_gnn_be2, "W3": L0_gnn_W3, "b3": L0_gnn_b3,
    }
    arrays = {k: np.ascontiguousarray(v) for k, v in arrays.items()}
    nc = bacc.Bacc("TRN2", target_bir_lowering=False, num_devices=1)
    aps = {k: nc.dram_tensor(f"in_{k}", v.shape, mybir.dt.from_np(v.dtype), kind="ExternalInput").ap()
           for k, v in arrays.items()}
    o = nc.dram_tensor("out", arrays["x"].shape, F32, kind="ExternalOutput").ap()
    build(nc, **aps, out=o)
    r = run_bass_kernel_spmd(nc, [{f"in_{k}": v for k, v in arrays.items()}], core_ids=[0])
    return r.results[0]["out"]
```

```python
from contextlib import ExitStack

import concourse.bass as bass
from concourse import mybir

F32, I32, U32, BF16 = mybir.dt.float32, mybir.dt.int32, mybir.dt.uint32, mybir.dt.bfloat16
ALU, ACT, AX = mybir.AluOpType, mybir.ActivationFunctionType, mybir.AxisListType

P = 128
EPS = 1e-5
WIN = 128
GT = 4
GE = GT * P
EA_GROUPS = 4
EA_SLOTS = 2
M_SLOTS = 4
NODE_SLOTS = 3
SMALLEST = 1e-20
ZERO_COLS = 1024


def ceil_div(a, b):
    return -(-a // b)


def build(nc, x, src_main, src_tail, dst_main, dst_tail, dst, eaT, W1, b1, g1, be1, W2, b2, g2, be2, W3, b3, out):
    N, NF = x.shape
    EF, E = eaT.shape
    L = W1.shape[1]
    D2 = W2.shape[0]
    assert NF == P and L == 2 * P and D2 == NF + L + 1
    KC = D2 // P
    GF = E // GE
    TAIL = E - GF * GE
    assert 0 < TAIL <= P and src_main.shape[1] == GF * GT
    NG = GF + 1
    TCOLS = GF * GT + 1
    BN_ = 4 * P
    EW = max(TCOLS, 3 * BN_)
    NH = ceil_div(N, P)
    NPAD = max(N + WIN, NH * P, 9600)
    NB = ceil_div(N, BN_)
    XC = 5
    NXC = ceil_div(NB, XC)
    GC = ceil_div(NG, P)
    EAU = ceil_div(NG, EA_GROUPS)
    assert NH <= P and KC == 3 and NB >= 2

    JOBS = [(b, c) for b in range(NB) for c in range(KC + 1)]
    job_group = [2 + j * (NG - 6) // len(JOBS) for j in range(len(JOBS))]
    job_of = {g: j for j, g in enumerate(job_group)}
    assert len(job_of) == len(JOBS) and job_group[-1] + 1 < NG

    def block_nodes(b):
        return min(BN_, N - b * BN_)

    def tiles_of(b):
        return [(t, b * BN_ + t * P, min(P, N - b * BN_ - t * P)) for t in range(ceil_div(block_nodes(b), P))]

    def tiles(g):
        return GT if g < GF else 1

    def rows(g):
        return P if g < GF else TAIL

    P1_d = nc.dram_tensor("P1_d", (N, L), F32, kind="Internal").ap()
    hT_d = nc.dram_tensor("hT_d", (P, N), F32, kind="Internal").ap()
    m_d = nc.dram_tensor("m_d", (NG, P, GT * L), F32, kind="Internal").ap()
    range_d = nc.dram_tensor("range_d", (2 * GC, P), F32, kind="Internal").ap()
    cnt_d = nc.dram_tensor("cnt_d", (2, NH, P), F32, kind="Internal").ap()
    early_d = nc.dram_tensor("early_d", (KC + 1, P, N), F32, kind="Internal").ap()
    odd_d = nc.dram_tensor("odd_d", (1, N), F32, kind="Internal").ap()

    with ExitStack() as ctx:
        def sb(name, shape, dt=F32):
            return ctx.enter_context(nc.sbuf_tensor(name, shape, dt))

        def sem(name):
            return ctx.enter_context(nc.semaphore(name))

        sums = sb("sums", [P, 2, NPAD])
        area = sb("area", [P, max(N, 12288)])
        flat = sums[:, :, :].rearrange("p a n -> p (a n)")
        x_all = flat[:, 0:NB * BN_].rearrange("p (t f) -> p t f", f=NF)
        taken = [NB * BN_]

        def early(cols, parts=P):
            a = taken[0]
            taken[0] += cols
            assert taken[0] <= 2 * NPAD
            return flat[0:parts, a:a + cols]

        grp = early(GC * GE)
        grp_f = grp[:, 0:GC * GE].rearrange("p (c e) -> p c e", c=GC)
        grp_i = grp[:, 0:GC * GE].bitcast(I32).rearrange("p (c e) -> p c e", c=GC)
        h_row = [area[:, 512 * i:512 * i + 512].rearrange("p (t f) -> p t f", t=4) for i in range(2)]
        hT_s = [area[:, 1024 + 512 * i:1536 + 512 * i] for i in range(2)]
        p1_s = [area[:, 2048 + 1024 * i:3072 + 1024 * i].rearrange("p (t f) -> p t f", t=4) for i in range(2)]
        m_s = [area[:, 1024 * i:1024 * i + 1024] for i in range(M_SLOTS)]
        q_s = [area[:, 4096 + 1024 * i:5120 + 1024 * i] for i in range(2)]
        ea_s = [area[0:EF, 6144 + 2048 * i:8192 + 2048 * i] for i in range(EA_SLOTS)]
        hT_j = [area[:, 10240 + 512 * i:10752 + 512 * i] for i in range(2)]
        part_s = [area[:, 11264 + 512 * i:11776 + 512 * i] for i in range(2)]
        plane = [sums[:, 0, :], sums[:, 1, :], area[:, :]]

        edges = sb("edges", [P, 4 * EW])
        idx = edges[:, 0:TCOLS].bitcast(I32)
        dst_f = edges[:, EW:EW + TCOLS]
        dst_hi = edges[:, 2 * EW:2 * EW + TCOLS]
        dst_lo = edges[:, 3 * EW:3 * EW + TCOLS]
        dst_hi_i, dst_lo_i = dst_hi.bitcast(I32), dst_lo.bitcast(I32)
        slots = edges[:, 0:12 * BN_].rearrange("p (s n) -> p s n", n=BN_)
        cnt_bc = [slots[:, i, :] for i in range(2)]
        inv_bc = [slots[:, 2 + i, :] for i in range(2)]
        part = [slots[:, 4 + 2 * i:6 + 2 * i, :] for i in range(2)]
        part_odd = [slots[0:1, 8 + i, :] for i in range(2)]
        odd_o = [slots[0:1, 10 + i, :] for i in range(2)]
        x_n = [slots[:, i, :].rearrange("p (t f) -> p t f", t=4) for i in range(NODE_SLOTS)]
        o_n = [slots[:, 3 + i, :].rearrange("p (t f) -> p t f", t=4) for i in range(NODE_SLOTS)]
        odd_i = [slots[0:1, 6 + i, :] for i in range(NODE_SLOTS)]
        odd_x = slots[0:2, 9:9 + NODE_SLOTS, :]
        at = 6144
        MEAN, EX2, VAR, SD, RS, A, C, INV, NEGT = range(9)
        bn_row = area[:, at:at + 9 * L].rearrange("p (s f) -> p s f", f=L)
        at += 9 * L
        sel = area[:, at:at + 4 * GT * WIN].rearrange("p (s k w) -> p s k w", s=4, k=GT)
        at += 4 * GT * WIN
        dist = area[:, at:at + 2 * GT * WIN].rearrange("p (s k w) -> p s k w", s=2, k=GT)
        assert at + 2 * GT * WIN <= 12288

        ident = sb("ident", [P, P])
        iota = sb("iota", [P, P])
        iota_b = sb("iota_b", [P, P], BF16)
        ones = sb("ones", [P, P])
        eps = sb("eps", [P, 1])
        bcol = sb("bcol", [P, 1])
        W1a = sb("W1a", [P, L])
        W1c = sb("W1c", [EF, L])
        b1_bc = sb("b1_bc", [P, L])
        W1b_bc = early(L)
        sgn = early(L)
        g1_bc, be1_bc = sb("g1_bc", [P, L]), sb("be1_bc", [P, L])
        W2s = sb("W2s", [P, 3, D2])
        W3s = sb("W3s", [P, KC, NF])
        W3o = sb("W3o", [2, NF])
        g2c, be2c, b2c, W2bc = (sb(n, [P, KC + 1]) for n in ("g2c", "be2c", "b2c", "W2bc"))
        ln_st = early(24 * NB).rearrange("p (t s) -> p t s", s=6)
        ln_mv = early(8 * NB).rearrange("p (t s) -> p t s", s=2)
        ln_r = early(4 * NB)
        ln_b = early(4 * NB)
        rng = sb("rng", [P, 2 * GC])
        rngT = sb("rngT", [2 * GC, P])
        base_bc = early(GC * P)
        rng_row = early(2 * GC * P, 1)
        base_i = sb("base_i", [1, GC * P], I32)
        wide = sb("wide", [1, 1])
        wide_i = sb("wide_i", [1, 1], I32)
        hot_hi = sb("hot_hi", [P, 2, GT, P], BF16)
        hot_lo = sb("hot_lo", [P, 2, GT, P], BF16)
        m_pair = sb("m_pair", [P, 2, 2 * L])
        a_col = sb("a_col", [P, 2])
        negt_col = sb("negt_col", [P, 2])
        T = sb("T", [P, L])
        cnt_s = sb("cnt_s", [NH, 2, P])
        bn2_st = sb("bn2_st", [P, KC + 1, NB, 6])
        bn2_mv = sb("bn2_mv", [P, KC + 1, 2])
        bn2 = sb("bn2", [P, 4, KC + 1])
        fb_sel = q_s[1][:, 0:GT * P].rearrange("p (k w) -> p k w", k=GT)
        fb_hi, fb_lo, fb_eq = sb("fb_hi", [P, GT]), sb("fb_lo", [P, GT]), sb("fb_eq", [P, GT])
        fb_w, fb_t = sb("fb_w", [P, 1]), sb("fb_t", [P, 1])

        psum = ctx.enter_context(nc.psum_tensor("psum", [P, 8, 512], F32))
        ps_m = [psum[:, 2 * i:2 * i + 2, :].rearrange("p a b -> p (a b)") for i in range(2)]
        ps_sum, ps_sq, ps_cnt, ps_col = psum[:, 4, :], psum[:, 6, :], psum[:, 5, :], psum[:, 7, :]
        ps_seg = [psum[:, i, 0:2 * WIN] for i in range(3)]
        ps_job = psum[:, 7, :]

        s_const = sem("s_const")
        s_w = sem("s_w")
        s_wp = sem("s_wp")
        s_x = [sem(f"s_x{i}") for i in range(NXC)]
        s_ei = sem("s_ei")
        s_grp = sem("s_grp")
        s_ei0 = sem("s_ei0")
        s_v = sem("s_v")
        s_sgn = sem("s_sgn")
        s_lnmv = sem("s_lnmv")
        s_lnsd = sem("s_lnsd")
        s_lnr = sem("s_lnr")
        s_h = sem("s_h")
        s_hT = sem("s_hT")
        s_hTs = sem("s_hTs")
        s_p1m = sem("s_p1m")
        s_p1 = sem("s_p1")
        s_p1w = [sem(f"s_p1w{i}") for i in range(2)]
        s_rng, s_rngT, s_rngs, s_rngw, s_rngl = (sem(n) for n in ("s_rng", "s_rngT", "s_rngs", "s_rngw", "s_rngl"))
        s_flag = sem("s_flag")
        s_gat = [[sem(f"s_gat{i}_{k}") for k in range(GT)] for i in range(M_SLOTS)]
        s_ea = [sem(f"s_ea{i}") for i in range(EA_SLOTS)]
        s_eam = sem("s_eam")
        s_m = sem("s_m")
        s_q = sem("s_q")
        s_hot = sem("s_hot")
        s_cnt = sem("s_cnt")
        s_pm = sem("s_pm")
        s_pq = sem("s_pq")
        s_st = sem("s_st")
        s_mw = [sem(f"s_mw{i}") for i in range(M_SLOTS)]
        s_hj = [sem(f"s_hj{i}") for i in range(2)]
        s_job = sem("s_job")
        s_jobs = sem("s_jobs")
        s_jobw = [sem(f"s_jobw{i}") for i in range(2)]
        s_var = sem("s_var")
        s_sd = sem("s_sd")
        s_row = sem("s_row")
        s_col = sem("s_col")
        s_cnts = sem("s_cnts")
        s_cntw = sem("s_cntw")
        s_ml = [sem(f"s_ml{i}") for i in range(M_SLOTS)]
        s_r = sem("s_r")
        s_sel = sem("s_sel")
        s_dist = sem("s_dist")
        s_seg = sem("s_seg")
        s_add = sem("s_add")
        s_B = sem("s_B")
        fb_free, fb_ld, fb_m, fb_e, fb_s, fb_pe, fb_add, fb_wc = (
            sem(n) for n in ("fb_free", "fb_ld", "fb_m", "fb_e", "fb_s", "fb_pe", "fb_add", "fb_wc"))
        s_hTl = [sem(f"s_hTl{i}") for i in range(NXC)]
        s_cl = [sem(f"s_cl{i}") for i in range(2)]
        s_pl = [sem(f"s_pl{i}") for i in range(2)]
        s_n00 = sem("s_n00")
        s_n0 = sem("s_n0")
        s_n1 = sem("s_n1")
        s_n1s = sem("s_n1s")
        s_ow = [sem(f"s_ow{i}") for i in range(2)]
        s_ol = [sem(f"s_ol{i}") for i in range(NODE_SLOTS)]
        s_bst = sem("s_bst")
        s_v2, s_sd2, s_c2 = sem("s_v2"), sem("s_sd2"), sem("s_c2")
        s_ones = sem("s_ones")
        s_r2 = sem("s_r2")
        s_n2 = sem("s_n2")
        s_xn = [sem(f"s_xn{i}") for i in range(NODE_SLOTS)]
        s_o = sem("s_o")
        s_out = [sem(f"s_out{i}") for i in range(NODE_SLOTS)]

        block = ctx.enter_context(nc.Block())

        def row_tiles_dma(eng, dram, sbuf, b, to_sbuf, done):
            n = block_nodes(b)
            full = n // P
            parts = []
            if full:
                parts.append((dram[b * BN_:b * BN_ + full * P, :].rearrange("(t p) f -> p t f", p=P), sbuf[:, 0:full, :]))
            if n % P:
                parts.append((dram[b * BN_ + full * P:b * BN_ + n, :], sbuf[0:n % P, full, :]))
            for d, s in parts:
                eng.dma_start(s if to_sbuf else d, d if to_sbuf else s).then_inc(done, 16)
            return len(parts)

        def row_parts(b):
            n = block_nodes(b)
            return (1 if n // P else 0) + (1 if n % P else 0)

        def space_of_windows_free(eng):
            eng.wait_ge(s_job, len(JOBS))
            for j in (len(JOBS) - 2, len(JOBS) - 1):
                eng.wait_ge(s_jobw[j % 2], 16 * (j // 2 + 1))

        def slot_count(b, per, slots=2):
            return 16 * sum(per(i) for i in range(b % slots, b + 1, slots))

        def table_written(eng):
            for b in (NB - 2, NB - 1):
                eng.wait_ge(s_p1w[b % 2], slot_count(b, lambda i: 1 + row_parts(i)))

        x_parts = [sum(row_parts(b) for b in range(c * XC, min(NB, c * XC + XC))) for c in range(NXC)]
        W_LOADS, COLUMN_LOADS = 12, 8

        @block.sync
        def _(sp):
            for c in range(NXC):
                for b in range(c * XC, min(NB, c * XC + XC)):
                    row_tiles_dma(sp, x, x_all[:, 4 * b:4 * b + 4, :], b, True, s_x[c])
                if c == 0:
                    loads = [(W1a[:, :], W1[0:NF, :]), (W1c[:, :], W1[NF + 1:, :]),
                             (b1_bc[:, :], b1.partition_broadcast(P)), (W1b_bc[:, :], W1[NF, :].partition_broadcast(P)),
                             (g1_bc[:, :], g1.partition_broadcast(P)), (be1_bc[:, :], be1.partition_broadcast(P)),
                             (W2s[:, 0, :], W2[0:NF, :]), (W2s[:, 1, :], W2[NF + 1:NF + 1 + P, :]),
                             (W2s[:, 2, :], W2[NF + 1 + P:, :]),
                             (W3s[:, :, :], W3[0:KC * P, :].rearrange("(c p) f -> p c f", p=P)),
                             (W3o[0:1, :], W3[KC * P:, :]), (W3o[1:2, :], b3.rearrange("(a f) -> a f", a=1))]
                    for d, s in loads:
                        sp.dma_start(d, s).then_inc(s_w, 16)
            sp.wait_ge(s_ei0, 3)
            sp.dma_start(idx[:, 0:TCOLS - 1], src_main).then_inc(s_ei, 16)
            sp.dma_start(idx[0:TAIL, TCOLS - 1:], src_tail).then_inc(s_ei, 16)
            sp.dma_start(dst_hi_i[:, 0:TCOLS - 1], dst_main).then_inc(s_ei, 16)
            sp.dma_start(dst_hi_i[0:TAIL, TCOLS - 1:], dst_tail).then_inc(s_ei, 16)
            for c in range(GC):
                n = min(P, GF - c * P)
                sp.dma_start(grp_i[0:n, c, :], dst[c * GE * P:(c * P + n) * GE].rearrange("(g e) -> g e", e=GE)).then_inc(s_grp, 16)
            sp.dma_start(grp_i[GF % P:GF % P + 1, GF // P, :], dst[E - GE:E].rearrange("(g e) -> g e", g=1)).then_inc(s_grp, 16)

            def load_ea(u):
                if u >= EA_SLOTS:
                    sp.wait_ge(s_eam, EA_GROUPS * (u - EA_SLOTS + 1))
                a = u * EA_GROUPS * GE
                n = min(EA_GROUPS * GE, E - a)
                sp.dma_start(ea_s[u % EA_SLOTS][:, 0:n], eaT[:, a:a + n]).then_inc(s_ea[u % EA_SLOTS], 16)
            for u in range(min(EA_SLOTS, EAU)):
                load_ea(u)
            for b in range(NB):
                n = block_nodes(b)
                sp.wait_ge(s_hTs, b + 1)
                sp.dma_start(hT_d[:, b * BN_:b * BN_ + n], hT_s[b % 2][:, 0:n]).then_inc(s_p1w[b % 2], 16)
                sp.wait_ge(s_p1, b + 1)
                row_tiles_dma(sp, P1_d, p1_s[b % 2], b, False, s_p1w[b % 2])
            sp.wait_ge(s_rngs, 1)
            sp.dma_start(range_d, rngT[:, :]).then_inc(s_rngw, 16)
            sp.wait_ge(s_rngw, 16)
            sp.dma_start(base_bc[:, :], range_d[0:GC, :].rearrange("c p -> (c p)").partition_broadcast(P)).then_inc(s_rngl, 16)
            sp.dma_start(rng_row[:, :], range_d.rearrange("(a c) p -> a (c p)", a=1)).then_inc(s_rngl, 16)
            def load_h(b):
                if b >= 2:
                    sp.wait_ge(s_job, (KC + 1) * (b - 1))
                n = block_nodes(b)
                sp.dma_start(hT_j[b % 2][:, 0:n], hT_d[:, b * BN_:b * BN_ + n]).then_inc(s_hj[b % 2], 16)

            def store_part(j):
                b, c = JOBS[j]
                n, mo = block_nodes(b), P if c < KC else 1
                sp.wait_ge(s_jobs, j + 1)
                sp.dma_start(early_d[c, 0:mo, b * BN_:b * BN_ + n], part_s[j % 2][0:mo, 0:n]).then_inc(s_jobw[j % 2], 16)

            table_written(sp)
            load_h(0)
            for g in range(NG):
                u = g // EA_GROUPS + 1
                if g % EA_GROUPS == EA_GROUPS - 1 and u + EA_SLOTS - 1 < EAU:
                    load_ea(u + EA_SLOTS - 1)
                sp.wait_ge(s_m, g + 1)
                r, w = rows(g), tiles(g) * L
                sp.dma_start(m_d[g, 0:r, 0:w], m_s[g % M_SLOTS][0:r, 0:w]).then_inc(s_mw[g % M_SLOTS], 16)
                if g - 1 in job_of:
                    store_part(job_of[g - 1])
                    b, c = JOBS[job_of[g - 1]]
                    if c == 0 and b + 1 < NB:
                        load_h(b + 1)
            sp.wait_ge(s_cnts, 1)
            sp.dma_start(cnt_d.rearrange("a h p -> h a p"), cnt_s[:, :, :]).then_inc(s_cntw, 16)
            for s in range(M_SLOTS):
                sp.wait_ge(s_mw[s], 16 * len(range(s, NG, M_SLOTS)))
            sp.wait_ge(s_st, NG)
            sp.wait_ge(s_q, NG)
            sp.wait_ge(s_flag, 1)
            flag = sp.alloc_register("wide_sp")
            sp.load(flag, wide_i[0:1, 0:1])
            with sp.If_eq(flag, 0):
                for g in range(NG):
                    if g >= M_SLOTS:
                        sp.wait_ge(s_seg, g - M_SLOTS + 1)
                    r, w = rows(g), tiles(g) * L
                    sp.dma_start(m_s[g % M_SLOTS][0:r, 0:w], m_d[g, 0:r, 0:w]).then_inc(s_ml[g % M_SLOTS], 16)
            with sp.Else():
                with sp.Fori(0, GF) as g:
                    sp.wait_ge(fb_free, g + 1)
                    sp.dma_start(m_s[0], m_d[bass.ds(g, 1), :, :].rearrange("g p w -> p (g w)")).then_inc(fb_ld, 16)
                sp.wait_ge(fb_free, GF + 1)
                sp.dma_start(m_s[0][0:TAIL, 0:L], m_d[GF, 0:TAIL, 0:L]).then_inc(fb_ld, 16)

            sp.wait_ge(s_B, 1)
            for j in (len(JOBS) - 2, len(JOBS) - 1):
                sp.wait_ge(s_jobw[j % 2], 16 * (j // 2 + 1))
            sp.wait_ge(s_cntw, 16)
            flat_cnt = cnt_d.rearrange("a h p -> a (h p)")
            for b in range(NB):
                n, c0 = block_nodes(b), b * BN_
                if b % XC == 0:
                    z = min(N, c0 + XC * BN_)
                    sp.dma_start(area[:, c0:z], early_d[2, :, c0:z]).then_inc(s_hTl[b // XC], 16)
                if b >= 2:
                    sp.wait_ge(s_n0, b - 1)
                for a, d in ((0, cnt_bc), (1, inv_bc)):
                    sp.dma_start(d[b % 2][:, 0:n], flat_cnt[a, c0:c0 + n].partition_broadcast(P)).then_inc(s_cl[b % 2], 16)
                if b >= 2:
                    sp.wait_ge(s_n1s, b - 1)
                sp.dma_start(part[b % 2][:, :, 0:n], early_d[0:2, :, c0:c0 + n].rearrange("c p n -> p c n")).then_inc(s_pl[b % 2], 16)
                sp.dma_start(part_odd[b % 2][:, 0:n], early_d[KC, 0:1, c0:c0 + n]).then_inc(s_pl[b % 2], 16)
            for i in range(2):
                sp.wait_ge(s_ow[i], 16 * len(range(i, NB, 2)))
            sp.wait_ge(s_n0, NB)
            sp.wait_ge(s_bst, NB)
            for b in range(NB):
                i, n = b % NODE_SLOTS, block_nodes(b)
                if b >= NODE_SLOTS:
                    sp.wait_ge(s_o, b - NODE_SLOTS + 1)
                    sp.wait_ge(s_r2, b - NODE_SLOTS + 1)
                row_tiles_dma(sp, x, x_n[i], b, True, s_xn[i])
                sp.dma_start(odd_i[i][:, 0:n], odd_d[:, b * BN_:b * BN_ + n]).then_inc(s_ol[i], 16)

        @block.gpsimd
        def _(pool):
            pool.memset(idx[:, TCOLS - 1:], 0).then_inc(s_ei0, 1)
            pool.memset(dst_hi_i[:, TCOLS - 1:], 0).then_inc(s_ei0, 1)
            pool.memset(grp_i, 0).then_inc(s_ei0, 1)
            pool.memset(ident[:, :], 0.0).then_inc(s_const, 1)
            pool.iota(iota[:, :], pattern=[[1, P]], base=0, channel_multiplier=0,
                      allow_small_or_imprecise_dtypes=True).then_inc(s_const, 1)
            pool.iota(iota_b[:, :], pattern=[[1, P]], base=0, channel_multiplier=0,
                      allow_small_or_imprecise_dtypes=True).then_inc(s_const, 1)
            pool.memset(ones[:, :], 1.0).then_inc(s_const, 1)
            pool.memset(eps[:, :], EPS).then_inc(s_const, 1)
            pool.memset(bcol[:, :], 0.0).then_inc(s_const, 1)
            pool.wait_ge(s_const, 6)
            pool.affine_select(out=ident[:, :], in_=ident[:, :], compare_op=ALU.not_equal, fill=1.0, base=0,
                               pattern=[[-1, P]], channel_multiplier=1).then_inc(s_const, 1)
            with nc.allow_non_contiguous_dma(reason="a few hundred parameters, once"):
                for v, c in ((g2, g2c), (be2, be2c), (b2, b2c), (W2[NF, :], W2bc)):
                    pool.dma_start(c[:, 0:KC], v[0:KC * P].rearrange("(c p) -> p c", p=P)).then_inc(s_wp, 16)
                    pool.dma_start(c[0:1, KC:], v[KC * P:].rearrange("(c p) -> p c", p=1)).then_inc(s_wp, 16)
            pool.wait_ge(s_ei, 64)
            table_written(pool)
            for g in range(NG):
                s, r = g % M_SLOTS, rows(g)
                if g >= M_SLOTS:
                    pool.wait_ge(s_mw[s], 16 * (g // M_SLOTS))
                    pool.wait_ge(s_pm, g - M_SLOTS + 1)
                    pool.wait_ge(s_q, g - M_SLOTS + 1)
                for k in range(tiles(g)):
                    pool.indirect_dma_start(
                        out=m_s[s][0:r, k * L:(k + 1) * L], out_offset=None, in_=P1_d,
                        in_offset=bass.IndirectOffsetOnAxis(ap=idx[0:r, GT * g + k:GT * g + k + 1].bitcast(U32), axis=0),
                    ).then_inc(s_gat[s][k], 16)
            def store_odd(b):
                n = block_nodes(b)
                pool.wait_ge(s_n1s, b + 1)
                pool.dma_start(odd_d[:, b * BN_:b * BN_ + n], odd_o[b % 2][:, 0:n]).then_inc(s_ow[b % 2], 16)

            for b in range(NB):
                n, c0 = block_nodes(b), b * BN_
                pool.wait_ge(s_n00, b + 1)
                v = sums[:, :, c0:c0 + n]
                pool.tensor_tensor(v, v, inv_bc[b % 2][:, 0:n].unsqueeze(1).to_broadcast([P, 2, n]), ALU.mult).then_inc(s_n0, 1)
                if b >= 2:
                    store_odd(b - 2)
            for b in (NB - 2, NB - 1):
                store_odd(b)
            for i in range(2):
                pool.wait_ge(s_ow[i], 16 * len(range(i, NB, 2)))
            pool.wait_ge(s_bst, NB)
            pool.memset(odd_x, 1.0).then_inc(s_ones, 1)
            for b in range(NB):
                pool.wait_ge(s_o, b + 1)
                row_tiles_dma(pool, out, o_n[b % NODE_SLOTS], b, False, s_out[b % NODE_SLOTS])
            for b in range(max(0, NB - NODE_SLOTS), NB):
                pool.wait_ge(s_out[b % NODE_SLOTS], slot_count(b, row_parts, NODE_SLOTS))

        @block.scalar
        def _(act):
            act.wait_ge(s_const, 7)

            def chunk_tiles(c):
                return 4 * XC * c, min(4 * NB, 4 * XC * (c + 1))

            def ln_sqrt(c):
                a, z = chunk_tiles(c)
                act.wait_ge(s_lnmv, c + 1)
                act.activation(ln_r[:, a:z], ln_mv[:, a:z, 1], ACT.Sqrt, bias=eps[:, 0:1]).then_inc(s_lnsd, 1)

            def h_rows(b):
                if b >= 2:
                    act.wait_ge(s_hT, b - 1)
                for t, a, r in tiles_of(b):
                    i = 4 * b + t
                    ins = act.activation(h_row[b % 2][0:r, t, :], x_all[0:r, i, :], ACT.Relu,
                                         bias=ln_b[0:r, i:i + 1], scale=ln_r[0:r, i:i + 1])
                ins.then_inc(s_h, 1)

            def hT_copy(b):
                n = block_nodes(b)
                act.wait_ge(s_hT, b + 1)
                if b >= 2:
                    act.wait_ge(s_p1w[b % 2], slot_count(b - 2, lambda i: 1 + row_parts(i)))
                    act.wait_ge(s_p1m, b - 1)
                act.activation(hT_s[b % 2][:, 0:n], psum[:, 6 + b % 2, 0:n], ACT.Copy).then_inc(s_hTs, 1)

            ln_sqrt(0)
            for b in range(NB):
                c = b // XC
                if b % XC == 0:
                    act.wait_ge(s_lnr, c + 1)
                h_rows(b)
                if b >= 1:
                    hT_copy(b - 1)
                if b % XC == 1 and c + 1 < NXC:
                    ln_sqrt(c + 1)
            hT_copy(NB - 1)
            for g in range(NG):
                r, w = rows(g), tiles(g) * L
                act.wait_ge(s_m, g + 1)
                if g >= 2:
                    act.wait_ge(s_st, g - 1)
                act.activation(q_s[g % 2][0:r, 0:w], m_s[g % M_SLOTS][0:r, 0:w], ACT.Square).then_inc(s_q, 1)
                if g in job_of:
                    j = job_of[g]
                    b, c = JOBS[j]
                    n, mo = block_nodes(b), P if c < KC else 1
                    act.wait_ge(s_job, j + 1)
                    if j >= 2:
                        act.wait_ge(s_jobw[j % 2], 16 * (j // 2))
                    act.activation(part_s[j % 2][0:mo, 0:n], ps_job[0:mo, 0:n], ACT.Identity,
                                   bias=b2c[0:mo, c:c + 1]).then_inc(s_jobs, 1)
            act.wait_ge(s_var, 1)
            act.activation(bn_row[:, SD, :], bn_row[:, VAR, :], ACT.Sqrt, bias=eps[:, 0:1]).then_inc(s_sd, 1)
            space_of_windows_free(act)
            flag = act.alloc_register("wide_act")
            act.wait_ge(s_flag, 1)
            act.load(flag, wide_i[0:1, 0:1])
            with act.If_eq(flag, 0):
                for g in range(NG):
                    r, nt = rows(g), tiles(g)
                    if g >= 2:
                        act.wait_ge(s_sel, g - 1)
                    for k in range(max(1, nt - 1)):
                        ins = act.activation(dist[0:r, g % 2, k, :], iota[0:r, 0:WIN], ACT.Abs,
                                             bias=dst_f[0:r, GT * g + k:GT * g + k + 1])
                    ins.then_inc(s_dist, 1)
                    act.wait_ge(s_dist, g + 1)
                    if g >= 4:
                        act.wait_ge(s_seg, g - 3)
                    na = max(1, nt - 1)
                    act.activation(sel[0:r, g % 4, 0:na, :], dist[0:r, g % 2, 0:na, :], ACT.Relu,
                                   bias=ones[0:r, 0:1], scale=-1.0).then_inc(s_sel, 1)
            with act.Else():
                pass
            act.wait_ge(s_v2, 1)
            act.activation(bn2[:, 0, 0:KC], bn2_mv[:, 0:KC, 1], ACT.Sqrt, bias=eps[:, 0:1])
            act.activation(bn2[0:1, 0, KC:], bn2_mv[0:1, KC:, 1], ACT.Sqrt, bias=eps[0:1, 0:1]).then_inc(s_sd2, 1)
            act.wait_ge(s_c2, 1)
            act.wait_ge(s_ones, 1)
            for b in range(NB):
                n, c0, i = block_nodes(b), b * BN_, b % NODE_SLOTS
                for c in range(KC):
                    act.activation(plane[c][:, c0:c0 + n], plane[c][:, c0:c0 + n], ACT.Relu,
                                   bias=bn2[:, 3, c:c + 1], scale=bn2[:, 2, c:c + 1])
                act.wait_ge(s_ol[i], 16 * (b // NODE_SLOTS + 1))
                if b >= NODE_SLOTS:
                    act.wait_ge(s_n2, b - NODE_SLOTS + 1)
                act.activation(odd_x[0:1, i, 0:n], odd_i[i][:, 0:n], ACT.Relu,
                               bias=bn2[0:1, 3, KC:], scale=bn2[0:1, 2, KC:]).then_inc(s_r2, 1)

        @block.vector
        def _(dve):
            steps = [0]

            def step(ins):
                steps[0] += 1
                ins.then_inc(s_v, 1)
                dve.wait_ge(s_v, steps[0])

            dve.wait_ge(s_const, 7)

            def ln_stats(c):
                lo, hi = c * XC, min(NB, c * XC + XC)
                dve.wait_ge(s_x[c], 16 * x_parts[c])
                tl = [(4 * b + t, r) for b in range(lo, hi) for t, _, r in tiles_of(b)]
                for i, r in tl:
                    ins = dve.bn_stats(ln_st[0:r, i, :], x_all[0:r, i, :])
                step(ins)
                for i, r in tl:
                    ins = dve.bn_aggr(ln_mv[0:r, i, :], ln_st[0:r, i, :])
                ins.then_inc(s_lnmv, 1)

            def ln_scale(c):
                a, z = 4 * XC * c, min(4 * NB, 4 * XC * (c + 1))
                dve.wait_ge(s_lnsd, c + 1)
                step(dve.reciprocal(ln_r[:, a:z], ln_r[:, a:z]))
                dve.scalar_tensor_tensor(ln_b[:, a:z], ln_mv[:, a:z, 0], -1.0, ln_r[:, a:z],
                                         ALU.mult, ALU.mult).then_inc(s_lnr, 1)

            dve.memset(ln_mv[:, :, :], 0.0)
            step(dve.memset(bn2_mv[:, :, :], 0.0))
            ln_stats(0)
            dve.wait_ge(s_w, 16 * W_LOADS)
            dve.wait_ge(s_wp, 16 * COLUMN_LOADS)
            step(dve.tensor_scalar(sgn[:, :], g1_bc[:, :], 0.0, 2.0, ALU.is_ge, ALU.mult))
            step(dve.tensor_scalar(sgn[:, :], sgn[:, :], -1.0, None, ALU.add))
            dve.tensor_tensor(g1_bc[:, :], g1_bc[:, :], sgn[:, :], ALU.mult)
            step(dve.scalar_tensor_tensor(b1_bc[:, :], W1b_bc[:, :], bcol[:, 0:1], b1_bc[:, :], ALU.mult, ALU.add))
            dve.tensor_tensor(b1_bc[:, :], b1_bc[:, :], sgn[:, :], ALU.mult)
            dve.tensor_tensor(W1a[:, :], W1a[:, :], sgn[:, :], ALU.mult)
            step(dve.tensor_tensor(W1c[:, :], W1c[:, :], sgn[0:EF, :], ALU.mult))
            dve.scalar_tensor_tensor(b2c[:, 0:KC], W2bc[:, 0:KC], bcol[:, 0:1], b2c[:, 0:KC], ALU.mult, ALU.add)
            dve.scalar_tensor_tensor(b2c[0:1, KC:], W2bc[0:1, KC:], bcol[0:1, 0:1], b2c[0:1, KC:],
                                     ALU.mult, ALU.add).then_inc(s_sgn, 1)

            def table_rows(b):
                dve.wait_ge(s_p1m, b + 1)
                if b >= 2:
                    dve.wait_ge(s_p1w[b % 2], slot_count(b - 2, lambda i: 1 + row_parts(i)))
                for t, _, r in tiles_of(b):
                    if t % 2 == 0:
                        n2 = min(2, len(tiles_of(b)) - t)
                        if all(q[2] == P for q in tiles_of(b)[t:t + n2]):
                            parts = [(t, n2, P)]
                        else:
                            parts = [(q[0], 1, q[2]) for q in tiles_of(b)[t:t + n2]]
                        for t0, m, rr in parts:
                            ins = dve.tensor_tensor(
                                p1_s[b % 2][0:rr, t0:t0 + m, :],
                                ps_m[b % 2][0:rr, t0 * L:(t0 + m) * L].rearrange("p (t f) -> p t f", f=L),
                                b1_bc[0:rr, :].unsqueeze(1).to_broadcast([rr, m, L]), ALU.add)
                ins.then_inc(s_p1, 1)

            ln_scale(0)
            if NXC > 1:
                ln_stats(1)
            for c in range(NXC):
                for b in range(c * XC, min(NB, c * XC + XC)):
                    table_rows(b)
                    if b % XC == 1 and c + 1 < NXC:
                        ln_scale(c + 1)
                    if b % XC == 2 and c + 2 < NXC:
                        ln_stats(c + 2)
                if c == 0:
                    dve.wait_ge(s_ei, 64)
                    dve.tensor_copy(dst_f[:, :], dst_hi_i[:, :])
                    step(dve.tensor_scalar(dst_lo_i[:, :], dst_hi_i[:, :], P - 1, None, ALU.bitwise_and))
                    step(dve.tensor_scalar(dst_hi_i[:, :], dst_hi_i[:, :], P.bit_length() - 1, None,
                                           ALU.logical_shift_right))
                    dve.tensor_copy(dst_hi, dst_hi_i[:, :])
                    step(dve.tensor_copy(dst_lo, dst_lo_i[:, :]))
                    dve.wait_ge(s_grp, 16 * (GC + 1))
                    step(dve.tensor_copy(grp_f, grp_i))
                    step(dve.tensor_reduce(rng[:, 0:GC], grp_f, AX.X, ALU.min))
                    step(dve.tensor_reduce(rng[:, GC:], grp_f, AX.X, ALU.max))
                    dve.tensor_tensor(rng[:, GC:], rng[:, GC:], rng[:, 0:GC], ALU.subtract).then_inc(s_rng, 1)
            dve.wait_ge(s_rngT, 1)
            dve.tensor_copy(rngT[:, :], psum[0:2 * GC, 5, 0:P]).then_inc(s_rngs, 1)
            dve.wait_ge(s_rngl, 32)

            def one_hot(g):
                if g >= 2:
                    dve.wait_ge(s_cnt, g - 1)
                r = rows(g)
                for k in range(tiles(g)):
                    j = GT * g + k
                    dve.tensor_scalar(hot_hi[0:r, g % 2, k, 0:NH], iota_b[0:r, 0:NH], dst_hi[0:r, j:j + 1], None, ALU.is_equal)
                    ins = dve.tensor_scalar(hot_lo[0:r, g % 2, k, :], iota_b[0:r, :], dst_lo[0:r, j:j + 1], None, ALU.is_equal)
                ins.then_inc(s_hot, 1)

            one_hot(0)
            dve.tensor_copy(base_i[:, :], rng_row[:, 0:GC * P])
            step(dve.tensor_reduce(wide[:, :], rng_row[:, GC * P:], AX.X, ALU.max))
            step(dve.tensor_scalar(wide[:, :], wide[:, :], float(WIN), None, ALU.is_ge))
            dve.tensor_copy(wide_i[:, :], wide[:, :])
            dve.tensor_tensor(dst_f[:, TCOLS - 1:], base_bc[:, GF:GF + 1], dst_f[:, TCOLS - 1:], ALU.subtract)
            main = dst_f[:, 0:GF * GT].rearrange("p (g k) -> p g k", k=GT)
            dve.tensor_tensor(main, base_bc[:, 0:GF].unsqueeze(2).to_broadcast([P, GF, GT]), main,
                              ALU.subtract).then_inc(s_flag, 1)
            zero_at = 0
            dve.wait_ge(s_h, NB)
            H2 = 2 * L
            for g in range(NG):
                s, r, w = g % M_SLOTS, rows(g), tiles(g) * L
                if zero_at < 2 * NPAD:
                    z = min(2 * NPAD, zero_at + ZERO_COLS)
                    dve.memset(flat[:, zero_at:z], 0.0)
                    zero_at = z
                if g >= 1:
                    dve.wait_ge(s_q, g)
                    q = q_s[(g - 1) % 2]
                    dve.tensor_tensor(q[:, 0:H2], q[:, 0:H2], q[:, H2:2 * H2], ALU.add).then_inc(s_pq, 1)
                for k in range(tiles(g)):
                    dve.wait_ge(s_gat[s][k], 16 * (g // M_SLOTS + 1))
                dve.wait_ge(s_eam, g + 1)
                dve.tensor_tensor(m_s[s][0:r, 0:w], ps_m[g % 2][0:r, 0:w], m_s[s][0:r, 0:w], ALU.add).then_inc(s_m, 1)
                if g + 1 < NG:
                    one_hot(g + 1)
                if g < GF:
                    dve.wait_ge(s_m, g + 1)
                    if g >= 2:
                        dve.wait_ge(s_st, g - 1)
                    dve.tensor_tensor(m_pair[:, g % 2, :], m_s[s][:, 0:H2], m_s[s][:, H2:2 * H2], ALU.add).then_inc(s_pm, 1)
            while zero_at < 2 * NPAD:
                z = min(2 * NPAD, zero_at + ZERO_COLS)
                step(dve.memset(flat[:, zero_at:z], 0.0))
                zero_at = z
            dve.wait_ge(s_st, NG)
            for ps, row in ((ps_sum, MEAN), (ps_sq, EX2)):
                step(dve.tensor_scalar(bn_row[:, row, :], ps[:, 0:L], 1.0 / E, None, ALU.mult))
                step(dve.scalar_tensor_tensor(bn_row[:, row, :], ps[:, L:2 * L], 1.0 / E, bn_row[:, row, :],
                                              ALU.mult, ALU.add))
            step(dve.tensor_tensor(bn_row[:, VAR, :], bn_row[:, MEAN, :], bn_row[:, MEAN, :], ALU.mult))
            step(dve.tensor_tensor(bn_row[:, VAR, :], bn_row[:, EX2, :], bn_row[:, VAR, :], ALU.subtract))
            dve.tensor_scalar(bn_row[:, VAR, :], bn_row[:, VAR, :], 0.0, None, ALU.max).then_inc(s_var, 1)
            dve.wait_ge(s_sd, 1)
            step(dve.reciprocal(bn_row[:, RS, :], bn_row[:, SD, :]))
            step(dve.tensor_tensor(bn_row[:, A, :], g1_bc[:, :], bn_row[:, RS, :], ALU.mult))
            step(dve.tensor_tensor(bn_row[:, C, :], bn_row[:, A, :], bn_row[:, MEAN, :], ALU.mult))
            step(dve.tensor_tensor(bn_row[:, C, :], be1_bc[:, :], bn_row[:, C, :], ALU.subtract))
            step(dve.tensor_scalar(bn_row[:, A, :], bn_row[:, A, :], SMALLEST, None, ALU.max))
            step(dve.reciprocal(bn_row[:, INV, :], bn_row[:, A, :]))
            dve.tensor_tensor(bn_row[:, NEGT, :], bn_row[:, C, :], bn_row[:, INV, :], ALU.mult).then_inc(s_row, 1)
            dve.wait_ge(s_row, 1)
            step(dve.tensor_scalar(T[:, :], bn_row[:, NEGT, :], -1.0, None, ALU.mult))
            dve.wait_ge(s_cnt, NG)
            step(dve.tensor_copy(cnt_s[:, 0, :], ps_cnt[0:NH, 0:P]))
            step(dve.tensor_scalar(cnt_s[:, 1, :], cnt_s[:, 0, :], 1.0, None, ALU.max))
            dve.reciprocal(cnt_s[:, 1, :], cnt_s[:, 1, :]).then_inc(s_cnts, 1)

            space_of_windows_free(dve)
            flag = dve.alloc_register("wide_dve")
            dve.load(flag, wide_i[0:1, 0:1])

            def clip(r, nt, slot):
                v = m_s[slot][0:r, 0:nt * L].rearrange("p (k f) -> p k f", f=L)
                return dve.tensor_tensor(v, v, T[0:r, :].unsqueeze(1).to_broadcast([r, nt, L]), ALU.max)

            with dve.If_eq(flag, 0):
                def add_window(g):
                    at = dve.value_load(base_i[0:1, g:g + 1], min_val=0, max_val=N - 1)
                    dve.wait_ge(s_seg, g + 1)
                    if g:
                        dve.wait_ge(s_add, g)
                    win = sums[:, :, bass.ds(at, WIN)]
                    dve.tensor_tensor(win, win, ps_seg[g % 3].rearrange("p (h w) -> p h w", h=2),
                                      ALU.add).then_inc(s_add, 1)
                for g in range(NG):
                    s = g % M_SLOTS
                    if g < GF:
                        if g >= 4:
                            dve.wait_ge(s_seg, g - 3)
                        dve.tensor_scalar(sel[:, g % 4, GT - 1, :], iota[:, :], dst_f[:, GT * g + GT - 1:GT * g + GT],
                                          0.0, ALU.add, ALU.is_equal)
                    dve.wait_ge(s_ml[s], 16 * (g // M_SLOTS + 1))
                    clip(rows(g), tiles(g), s).then_inc(s_r, 1)
                    if g >= 2:
                        add_window(g - 2)
                add_window(NG - 2)
                add_window(NG - 1)
                dve.wait_ge(s_add, NG)
                dve.memset(fb_t[:, :], 0.0).then_inc(s_B, 1)
            with dve.Else():
                def group(g, r, nt, first):
                    dve.wait_ge(fb_ld, (g + 1) * 16)
                    clip(r, nt, 0).then_inc(fb_m, 1)
                    if first is None:
                        dve.tensor_copy(fb_hi[0:r, 0:nt], dst_hi[0:r, TCOLS - 1:]).then_inc(fb_m, 1)
                        dve.tensor_copy(fb_lo[0:r, 0:nt], dst_lo[0:r, TCOLS - 1:]).then_inc(fb_m, 1)
                    else:
                        dve.tensor_copy(fb_hi[:, :], dst_hi[:, bass.ds(g * GT, GT)]).then_inc(fb_m, 1)
                        dve.tensor_copy(fb_lo[:, :], dst_lo[:, bass.ds(g * GT, GT)]).then_inc(fb_m, 1)
                    dve.memset(fb_w[:, :], 0.0).then_inc(fb_m, 1)
                    dve.wait_ge(fb_m, (g + 1) * 4)
                    dve.tensor_copy(fb_t[:, :], fb_w[:, :])
                    with dve.Fori(0, NH) as w:
                        i = g * NH + w
                        dve.tensor_scalar(fb_eq[0:r, 0:nt], fb_hi[0:r, 0:nt], fb_w[0:r, 0:1], None,
                                          ALU.is_equal).then_inc(fb_e, 1)
                        dve.wait_ge(fb_e, i + 1)
                        for k in range(nt):
                            ins = dve.tensor_scalar(fb_sel[0:r, k, :], iota[0:r, :], fb_lo[0:r, k:k + 1],
                                                    fb_eq[0:r, k:k + 1], ALU.is_equal, ALU.mult)
                        ins.then_inc(fb_s, 1)
                        dve.tensor_scalar(fb_w[:, :], fb_w[:, :], 1.0, None, ALU.add).then_inc(fb_wc, 1)
                        dve.wait_ge(fb_wc, i + 1)
                        dve.wait_ge(fb_pe, i + 1)
                        win = sums[:, :, bass.ds(w * P, P)]
                        dve.tensor_tensor(win, win, psum[:, 0, 0:2 * P].rearrange("p (h w) -> p h w", h=2),
                                          ALU.add).then_inc(fb_add, 1)
                        dve.wait_ge(fb_add, i + 1)
                    dve.memset(fb_t[:, :], 0.0).then_inc(fb_free, 1)
                dve.memset(fb_t[:, :], 0.0).then_inc(fb_free, 1)
                with dve.Fori(0, GF) as g:
                    group(g, P, GT, 0)
                group(GF, TAIL, 1, None)
                dve.wait_ge(fb_free, GF + 2)
                dve.memset(fb_t[:, :], 0.0).then_inc(s_B, 1)

            dve.wait_ge(s_col, 1)
            cols = ps_col.rearrange("p (v f) -> p v f", f=P)[:, :, 0]
            dve.tensor_copy(a_col[:, :], cols[:, 0:2])
            step(dve.tensor_copy(negt_col[:, :], cols[:, 2:4]))
            for h in range(2):
                step(dve.tensor_scalar(W2s[:, 1 + h, :], W2s[:, 1 + h, :], a_col[:, h:h + 1], None, ALU.mult))

            def centre(b):
                n, c0 = block_nodes(b), b * BN_
                dve.wait_ge(s_cl[b % 2], 32 * (b // 2 + 1))
                for h in range(2):
                    v = sums[:, h, c0:c0 + n]
                    ins = dve.scalar_tensor_tensor(v, cnt_bc[b % 2][:, 0:n], negt_col[:, h:h + 1], v, ALU.mult, ALU.add)
                ins.then_inc(s_n00, 1)

            def pre(b):
                n, c0, bank = block_nodes(b), b * BN_, 4 * (b % 2)
                dve.wait_ge(s_n1, b + 1)
                dve.wait_ge(s_hTl[b // XC], 16)
                dve.wait_ge(s_pl[b % 2], 32 * (b // 2 + 1))
                if b >= 2:
                    dve.wait_ge(s_ow[b % 2], 16 * (b // 2))
                for c, early in enumerate((part[b % 2][:, 0, 0:n], part[b % 2][:, 1, 0:n], area[:, c0:c0 + n])):
                    dve.tensor_tensor(plane[c][:, c0:c0 + n], psum[:, bank + c, 0:n], early, ALU.add)
                dve.tensor_tensor(odd_o[b % 2][:, 0:n], psum[0:1, bank + KC, 0:n], part_odd[b % 2][:, 0:n],
                                  ALU.add).then_inc(s_n1s, 1)
                dve.wait_ge(s_n1s, b + 1)
                for c in range(KC):
                    dve.bn_stats(bn2_st[:, c, b, :], plane[c][:, c0:c0 + n])
                dve.bn_stats(bn2_st[0:1, KC, b, :], odd_o[b % 2][:, 0:n]).then_inc(s_bst, 1)

            dve.wait_ge(s_B, 1)
            for b in range(NB):
                centre(b)
                if b >= 1:
                    pre(b - 1)
            pre(NB - 1)
            dve.wait_ge(s_bst, NB)
            for c in range(KC):
                dve.bn_aggr(bn2_mv[:, c, :], bn2_st[:, c, :, :].rearrange("p b s -> p (b s)"))
            dve.bn_aggr(bn2_mv[0:1, KC, :], bn2_st[0:1, KC, :, :].rearrange("p b s -> p (b s)")).then_inc(s_v2, 1)
            dve.wait_ge(s_sd2, 1)
            for p, a, z in ((P, 0, KC), (1, KC, KC + 1)):
                step(dve.reciprocal(bn2[0:p, 1, a:z], bn2[0:p, 0, a:z]))
                step(dve.tensor_tensor(bn2[0:p, 2, a:z], g2c[0:p, a:z], bn2[0:p, 1, a:z], ALU.mult))
                step(dve.tensor_tensor(bn2[0:p, 3, a:z], bn2[0:p, 2, a:z], bn2_mv[0:p, a:z, 0], ALU.mult))
                ins = dve.tensor_tensor(bn2[0:p, 3, a:z], be2c[0:p, a:z], bn2[0:p, 3, a:z], ALU.subtract)
                if p == P:
                    step(ins)
                else:
                    ins.then_inc(s_c2, 1)
            for b in range(NB):
                i = b % NODE_SLOTS
                dve.wait_ge(s_n2, b + 1)
                dve.wait_ge(s_xn[i], slot_count(b, row_parts, NODE_SLOTS))
                if b >= NODE_SLOTS:
                    dve.wait_ge(s_out[i], slot_count(b - NODE_SLOTS, row_parts, NODE_SLOTS))
                tl = tiles_of(b)
                full = sum(1 for q in tl if q[2] == P)
                parts = ([(0, full, P)] if full else []) + [(q[0], 1, q[2]) for q in tl if q[2] < P]
                for t0, m, r in parts:
                    ins = dve.scalar_tensor_tensor(
                        o_n[i][0:r, t0:t0 + m, :],
                        psum[0:r, b % 4, t0 * P:(t0 + m) * P].rearrange("p (t f) -> p t f", f=NF), 0.0,
                        x_n[i][0:r, t0:t0 + m, :], ALU.max, ALU.add)
                ins.then_inc(s_o, 1)

        @block.tensor
        def _(pe):
            pe.wait_ge(s_const, 7)
            pe.wait_ge(s_sgn, 1)

            def turn(b):
                pe.wait_ge(s_h, b + 1)
                if b >= 2:
                    pe.wait_ge(s_hTs, b - 1)
                for t, _, r in tiles_of(b):
                    ins = pe.transpose(psum[:, 6 + b % 2, t * P:t * P + r], h_row[b % 2][0:r, t, :], ident[0:r, 0:r])
                ins.then_inc(s_hT, 1)

            def table(b):
                pe.wait_ge(s_hTs, b + 1)
                if b >= 2:
                    pe.wait_ge(s_p1, b - 1)
                for t, _, r in tiles_of(b):
                    ins = pe.matmul(ps_m[b % 2][0:r, t * L:(t + 1) * L], hT_s[b % 2][:, t * P:t * P + r], W1a[:, :],
                                    start=True, stop=True)
                ins.then_inc(s_p1m, 1)

            for b in range(NB):
                turn(b)
                if b >= 1:
                    table(b - 1)
            table(NB - 1)
            pe.wait_ge(s_rng, 1)
            pe.transpose(psum[0:2 * GC, 5, 0:P], rng[:, :], ident[:, :]).then_inc(s_rngT, 1)
            pe.wait_ge(s_p1, NB)
            pe.wait_ge(s_rngs, 1)

            def stats(g):
                if g < GF:
                    pe.wait_ge(s_pm, g + 1)
                    pe.wait_ge(s_pq, g + 1)
                    r, w, m = P, 2 * L, m_pair[:, g % 2, :]
                else:
                    pe.wait_ge(s_q, g + 1)
                    r, w, m = TAIL, L, m_s[g % M_SLOTS]
                for ps, v in ((ps_sum, m), (ps_sq, q_s[g % 2])):
                    ins = pe.matmul(ps[:, 0:w], ones[0:r, :], v[0:r, 0:w], start=(g == 0), stop=(g == NG - 1),
                                    skip_group_check=True)
                ins.then_inc(s_st, 1)

            def early_part(j):
                b, c = JOBS[j]
                n, mo = block_nodes(b), P if c < KC else 1
                if c == 0:
                    pe.wait_ge(s_hj[b % 2], 16 * (b // 2 + 1))
                pe.wait_ge(s_jobs, j)
                pe.matmul(ps_job[0:mo, 0:n], W2s[:, 0, c * P:c * P + mo], hT_j[b % 2][:, 0:n],
                          start=True, stop=True).then_inc(s_job, 1)

            pe.wait_ge(s_hTs, NB)
            for g in range(NG):
                u, r = g // EA_GROUPS, rows(g)
                if g % EA_GROUPS == 0:
                    pe.wait_ge(s_ea[u % EA_SLOTS], 16 * (u // EA_SLOTS + 1))
                if g >= 2:
                    pe.wait_ge(s_m, g - 1)
                for k in range(tiles(g)):
                    a = (g % EA_GROUPS) * GE + k * P
                    ins = pe.matmul(ps_m[g % 2][0:r, k * L:(k + 1) * L], ea_s[u % EA_SLOTS][:, a:a + r], W1c[:, :],
                                    start=True, stop=True)
                ins.then_inc(s_eam, 1)
                pe.wait_ge(s_hot, g + 1)
                for k in range(tiles(g)):
                    ins = pe.matmul(ps_cnt[0:NH, 0:P], hot_hi[0:r, g % 2, k, 0:NH], hot_lo[0:r, g % 2, k, :],
                                    start=(g == 0 and k == 0), stop=(g == NG - 1), skip_group_check=True)
                ins.then_inc(s_cnt, 1)
                if g >= 1:
                    stats(g - 1)
                if g in job_of:
                    early_part(job_of[g])
            stats(NG - 1)
            pe.wait_ge(s_row, 1)
            pe.wait_ge(s_jobs, len(JOBS))
            for i, (v, h) in enumerate(((A, 0), (A, 1), (NEGT, 0), (NEGT, 1))):
                ins = pe.transpose(ps_col[:, i * P:(i + 1) * P], bn_row[:, v, h * P:(h + 1) * P], ident[:, :])
            ins.then_inc(s_col, 1)

            def window(nt, r, slot, sel_k, width, bank_ap, done):
                for k in range(nt):
                    for h in range(2):
                        ins = pe.matmul(bank_ap[:, h * width:(h + 1) * width],
                                        m_s[slot][0:r, k * L + h * P:k * L + (h + 1) * P], sel_k(k)[0:r, :],
                                        start=(k == 0 and h == 0), stop=(k == nt - 1), skip_group_check=True)
                ins.then_inc(done, 1)

            flag = pe.alloc_register("wide_pe")
            pe.wait_ge(s_flag, 1)
            pe.load(flag, wide_i[0:1, 0:1])
            with pe.If_eq(flag, 0):
                for g in range(NG):
                    pe.wait_ge(s_r, g + 1)
                    pe.wait_ge(s_sel, g + 1)
                    if g >= 3:
                        pe.wait_ge(s_add, g - 2)
                    window(tiles(g), rows(g), g % M_SLOTS, lambda k, g=g: sel[:, g % 4, k, :], WIN, ps_seg[g % 3], s_seg)
            with pe.Else():
                with pe.Fori(0, GF) as g:
                    with pe.Fori(0, NH) as w:
                        pe.wait_ge(fb_s, g * NH + w + 1)
                        window(GT, P, 0, lambda k: fb_sel[:, k, :], P, psum[:, 0, :], fb_pe)
                with pe.Fori(0, NH) as w:
                    pe.wait_ge(fb_s, w + (GF * NH + 1))
                    window(1, TAIL, 0, lambda k: fb_sel[:, k, :], P, psum[:, 0, :], fb_pe)

            for b in range(NB):
                n, c0 = block_nodes(b), b * BN_
                pe.wait_ge(s_n0, b + 1)
                if b >= 2:
                    pe.wait_ge(s_n1s, b - 1)
                for c in range(KC + 1):
                    mo = P if c < KC else 1
                    for h in range(2):
                        ins = pe.matmul(psum[0:mo, 4 * (b % 2) + c, 0:n], W2s[:, 1 + h, c * P:c * P + mo],
                                        plane[h][:, c0:c0 + n], start=(h == 0), stop=(h == 1))
                ins.then_inc(s_n1, 1)
            pe.wait_ge(s_n1s, NB)
            for b in range(NB):
                pe.wait_ge(s_r2, b + 1)
                if b >= 4:
                    pe.wait_ge(s_o, b - 3)
                for t, a, r in tiles_of(b):
                    o = psum[0:r, b % 4, t * P:(t + 1) * P]
                    for c in range(KC):
                        pe.matmul(o, plane[c][:, a:a + r], W3s[:, c, :], start=(c == 0), stop=False)
                    ins = pe.matmul(o, odd_x[0:2, b % NODE_SLOTS, t * P:t * P + r], W3o[:, :], start=False, stop=True)
                ins.then_inc(s_n2, 1)


def kernel(x, src, dst, edge_attr_64, L0_gnn_u, L0_gnn_W1, L0_gnn_b1, L0_gnn_g1, L0_gnn_be1, L0_gnn_W2,
           L0_gnn_b2, L0_gnn_g2, L0_gnn_be2, L0_gnn_W3, L0_gnn_b3):
    import numpy as np
    import concourse.bacc as bacc
    from concourse.bass_utils import run_bass_kernel_spmd

    src, dst = np.asarray(src), np.asarray(dst)
    full = src.shape[0] // GE * GE

    def columns(v):
        return np.ascontiguousarray(v[:full].reshape(-1, P).T), np.ascontiguousarray(v[full:].reshape(-1, 1))

    src_main, src_tail = columns(src)
    dst_main, dst_tail = columns(dst)
    arrays = {
        "x": x, "src_main": src_main, "src_tail": src_tail, "dst_main": dst_main, "dst_tail": dst_tail, "dst": dst,
        "eaT": np.ascontiguousarray(np.asarray(edge_attr_64).T),
        "W1": L0_gnn_W1, "b1": L0_gnn_b1, "g1": L0_gnn_g1, "be1": L0_gnn_be1,
        "W2": L0_gnn_W2, "b2": L0_gnn_b2, "g2": L0_gnn_g2, "be2": L0_gnn_be2, "W3": L0_gnn_W3, "b3": L0_gnn_b3,
    }
    arrays = {k: np.ascontiguousarray(v) for k, v in arrays.items()}
    nc = bacc.Bacc("TRN2", target_bir_lowering=False, num_devices=1)
    aps = {k: nc.dram_tensor(f"in_{k}", v.shape, mybir.dt.from_np(v.dtype), kind="ExternalInput").ap()
           for k, v in arrays.items()}
    o = nc.dram_tensor("out", arrays["x"].shape, F32, kind="ExternalOutput").ap()
    build(nc, **aps, out=o)
    r = run_bass_kernel_spmd(nc, [{f"in_{k}": v for k, v in arrays.items()}], core_ids=[0])
    return r.results[0]["out"]
```

```python
from contextlib import ExitStack

import concourse.bass as bass
from concourse import mybir

F32, I32, U32, BF16 = mybir.dt.float32, mybir.dt.int32, mybir.dt.uint32, mybir.dt.bfloat16
ALU, ACT, AX = mybir.AluOpType, mybir.ActivationFunctionType, mybir.AxisListType

P = 128
EPS = 1e-5
WIN = 128
GT = 4
GE = GT * P
EA_GROUPS = 4
EA_SLOTS = 2
M_SLOTS = 4
NODE_SLOTS = 3
ROW_SLOTS = 4
SMALLEST = 1e-20
ZERO_COLS = 1024


def ceil_div(a, b):
    return -(-a // b)


def build(nc, x, src_main, src_tail, dst_main, dst_tail, dst, eaT, W1, b1, g1, be1, W2, b2, g2, be2, W3, b3, out):
    N, NF = x.shape
    EF, E = eaT.shape
    L = W1.shape[1]
    D2 = W2.shape[0]
    assert NF == P and L == 2 * P and D2 == NF + L + 1
    KC = D2 // P
    GF = E // GE
    TAIL = E - GF * GE
    assert 0 < TAIL <= P and src_main.shape[1] == GF * GT
    NG = GF + 1
    TCOLS = GF * GT + 1
    BN_ = 4 * P
    EW = max(TCOLS, 3 * BN_)
    NH = ceil_div(N, P)
    NPAD = max(N + WIN, NH * P, 9600)
    NB = ceil_div(N, BN_)
    XC = 5
    XL = 2
    NXL = ceil_div(NB, XL)
    NXC = ceil_div(NB, XC)
    GC = ceil_div(NG, P)
    EAU = ceil_div(NG, EA_GROUPS)
    ODD_BANK = 4 * (NB % 2)
    assert NH <= P and KC == 3 and NB >= 2

    JOBS = [(b, c) for b in range(NB) for c in range(KC + 1)]
    RANGE, TURN, SEND, BACK = 1, 3, 5, 9
    job_group = [TURN + 3 + j * (NG - TURN - 7) // len(JOBS) for j in range(len(JOBS))]
    job_of = {g: j for j, g in enumerate(job_group)}
    assert len(job_of) == len(JOBS) and job_group[-1] + 1 < NG

    def block_nodes(b):
        return min(BN_, N - b * BN_)

    def tiles_of(b):
        return [(t, b * BN_ + t * P, min(P, N - b * BN_ - t * P)) for t in range(ceil_div(block_nodes(b), P))]

    def tiles(g):
        return GT if g < GF else 1

    def rows(g):
        return P if g < GF else TAIL

    P1_d = nc.dram_tensor("P1_d", (N, L), F32, kind="Internal").ap()
    m_d = nc.dram_tensor("m_d", (NG, P, GT * L), F32, kind="Internal").ap()
    range_d = nc.dram_tensor("range_d", (2 * GC, P), F32, kind="Internal").ap()
    cnt_d = nc.dram_tensor("cnt_d", (2, NH, P), F32, kind="Internal").ap()
    early_d = nc.dram_tensor("early_d", (KC, P, N), F32, kind="Internal").ap()

    with ExitStack() as ctx:
        def sb(name, shape, dt=F32):
            return ctx.enter_context(nc.sbuf_tensor(name, shape, dt))

        def sem(name):
            return ctx.enter_context(nc.semaphore(name))

        sums = sb("sums", [P, 2, NPAD])
        area = sb("area", [P, max(N, 12288)])
        flat = sums[:, :, :].rearrange("p a n -> p (a n)")
        x_all = flat[:, 0:NB * BN_].rearrange("p (t f) -> p t f", f=NF)
        taken = [NB * BN_]

        def early(cols, parts=P):
            a = taken[0]
            taken[0] += cols
            assert taken[0] <= 2 * NPAD
            return flat[0:parts, a:a + cols]

        grp = early(GC * GE)
        grp_f = grp[:, 0:GC * GE].rearrange("p (c e) -> p c e", c=GC)
        grp_i = grp[:, 0:GC * GE].bitcast(I32).rearrange("p (c e) -> p c e", c=GC)
        hT = [flat[:, BN_ * b:BN_ * b + BN_] for b in range(NB)]
        h_row = [early(BN_).rearrange("p (t f) -> p t f", t=4) for i in range(ROW_SLOTS)]
        p1_s = [area[:, 1024 * i:1024 * i + 1024].rearrange("p (t f) -> p t f", t=4) for i in range(ROW_SLOTS)]
        m_s = [area[:, 1024 * i:1024 * i + 1024] for i in range(M_SLOTS)]
        q_s = [area[:, 4096 + 1024 * i:5120 + 1024 * i] for i in range(2)]
        ea_s = [area[0:EF, 6144 + 2048 * i:8192 + 2048 * i] for i in range(EA_SLOTS)]
        part_s = [area[:, 11264 + 512 * i:11776 + 512 * i] for i in range(2)]
        plane = [sums[:, 0, :], sums[:, 1, :], area[:, :]]

        edges = sb("edges", [P, 4 * EW])
        idx = edges[:, 0:TCOLS].bitcast(I32)
        dst_f = edges[:, EW:EW + TCOLS]
        dst_hi = edges[:, 2 * EW:2 * EW + TCOLS]
        dst_lo = edges[:, 3 * EW:3 * EW + TCOLS]
        dst_hi_i, dst_lo_i = dst_hi.bitcast(I32), dst_lo.bitcast(I32)
        slots = edges[:, 0:12 * BN_].rearrange("p (s n) -> p s n", n=BN_)
        cnt_bc = [slots[:, 2 * i, :] for i in range(2)]
        inv_bc = [slots[:, 1 + 2 * i, :] for i in range(2)]
        part = [slots[:, 4 + 2 * i:6 + 2 * i, :] for i in range(2)]
        x_n = [slots[:, i, :].rearrange("p (t f) -> p t f", t=4) for i in range(NODE_SLOTS)]
        o_n = [slots[:, 3 + i, :].rearrange("p (t f) -> p t f", t=4) for i in range(NODE_SLOTS)]
        at = 6144
        MEAN, EX2, VAR, SD, RS, A, C, INV, NEGT = range(9)
        bn_row = area[:, at:at + 9 * L].rearrange("p (s f) -> p s f", f=L)
        at += 9 * L
        sel = area[:, at:at + 4 * GT * WIN].rearrange("p (s k w) -> p s k w", s=4, k=GT)
        at += 4 * GT * WIN
        dist = area[:, at:at + 2 * GT * WIN].rearrange("p (s k w) -> p s k w", s=2, k=GT)
        assert at + 2 * GT * WIN <= 12288

        ident = sb("ident", [P, P])
        iota = sb("iota", [P, P])
        iota_b = sb("iota_b", [P, P], BF16)
        ones = sb("ones", [P, P])
        eps = sb("eps", [P, 1])
        bcol = sb("bcol", [P, 1])
        W1a = sb("W1a", [P, L])
        W1c = sb("W1c", [EF, L])
        b1_bc = sb("b1_bc", [P, L])
        W1b_bc = early(L)
        sgn = early(L)
        g1_bc, be1_bc = sb("g1_bc", [P, L]), sb("be1_bc", [P, L])
        W2s = sb("W2s", [P, 3, D2])
        W3s = sb("W3s", [P, KC, NF])
        W3o_bc, b3_bc = sb("W3o_bc", [P, NF]), sb("b3_bc", [P, NF])
        odd = sb("odd", [P, 4 * NB])
        odd_sq = sb("odd_sq", [P, 4 * NB])
        odd_sum = sb("odd_sum", [P, 4])
        g2c, be2c, b2c, W2bc = (sb(n, [P, KC + 1]) for n in ("g2c", "be2c", "b2c", "W2bc"))
        ln_st = early(24 * NB).rearrange("p (t s) -> p t s", s=6)
        ln_mv = early(8 * NB).rearrange("p (t s) -> p t s", s=2)
        ln_r = early(4 * NB)
        ln_b = early(4 * NB)
        rng = sb("rng", [P, 2 * GC])
        rngT = sb("rngT", [2 * GC, P])
        base_bc = early(GC * P)
        rng_row = early(2 * GC * P, 1)
        base_i = sb("base_i", [1, GC * P], I32)
        wide = sb("wide", [1, 1])
        wide_i = sb("wide_i", [1, 1], I32)
        hot_hi = sb("hot_hi", [P, 2, GT, P], BF16)
        hot_lo = sb("hot_lo", [P, 2, GT, P], BF16)
        m_pair = sb("m_pair", [P, 2, 2 * L])
        a_col = sb("a_col", [P, 2])
        negt_col = sb("negt_col", [P, 2])
        T = sb("T", [P, L])
        cnt_s = sb("cnt_s", [NH, 2, P])
        bn2_st = sb("bn2_st", [P, KC, NB, 6])
        bn2_mv = sb("bn2_mv", [P, KC + 1, 2])
        bn2 = sb("bn2", [P, 4, KC + 1])
        fb_sel = q_s[1][:, 0:GT * P].rearrange("p (k w) -> p k w", k=GT)
        fb_hi, fb_lo, fb_eq = sb("fb_hi", [P, GT]), sb("fb_lo", [P, GT]), sb("fb_eq", [P, GT])
        fb_w, fb_t = sb("fb_w", [P, 1]), sb("fb_t", [P, 1])

        psum = ctx.enter_context(nc.psum_tensor("psum", [P, 8, 512], F32))
        ps_m = [psum[:, 2 * i:2 * i + 2, :].rearrange("p a b -> p (a b)") for i in range(2)]
        ps_sum, ps_sq, ps_cnt, ps_col = psum[:, 4, :], psum[:, 6, :], psum[:, 5, :], psum[:, 7, :]
        ps_seg = [psum[:, i, 0:2 * WIN] for i in range(3)]
        ps_job = psum[:, 7, :]

        s_const = sem("s_const")
        s_w1 = sem("s_w1")
        s_w = sem("s_w")
        s_wp = sem("s_wp")
        s_x = [sem(f"s_x{i}") for i in range(NXL)]
        s_ei = sem("s_ei")
        s_grp = sem("s_grp")
        s_ei0 = sem("s_ei0")
        s_v = sem("s_v")
        s_sgn = sem("s_sgn")
        s_lnmv = sem("s_lnmv")
        s_lnsd = sem("s_lnsd")
        s_lnr = sem("s_lnr")
        s_h = sem("s_h")
        s_hT = sem("s_hT")
        s_hTs = sem("s_hTs")
        s_p1m = sem("s_p1m")
        s_p1 = sem("s_p1")
        s_p1w = [sem(f"s_p1w{i}") for i in range(ROW_SLOTS)]
        s_rng, s_rngT, s_rngs, s_rngw, s_rngl = (sem(n) for n in ("s_rng", "s_rngT", "s_rngs", "s_rngw", "s_rngl"))
        s_flag = sem("s_flag")
        s_gat = [[sem(f"s_gat{i}_{k}") for k in range(GT)] for i in range(M_SLOTS)]
        s_ea = [sem(f"s_ea{i}") for i in range(EA_SLOTS)]
        s_eam = sem("s_eam")
        s_m = sem("s_m")
        s_q = sem("s_q")
        s_hot = sem("s_hot")
        s_cnt = sem("s_cnt")
        s_pm = sem("s_pm")
        s_pq = sem("s_pq")
        s_st = sem("s_st")
        s_mw = [sem(f"s_mw{i}") for i in range(M_SLOTS)]
        s_job = sem("s_job")
        s_jobs = sem("s_jobs")
        s_jobw = [sem(f"s_jobw{i}") for i in range(2)]
        s_var = sem("s_var")
        s_sd = sem("s_sd")
        s_row = sem("s_row")
        s_col = sem("s_col")
        s_cnts = sem("s_cnts")
        s_cntw = sem("s_cntw")
        s_ml = [sem(f"s_ml{i}") for i in range(M_SLOTS)]
        s_r = sem("s_r")
        s_sel = sem("s_sel")
        s_dist = sem("s_dist")
        s_seg = sem("s_seg")
        s_add = sem("s_add")
        s_B = sem("s_B")
        fb_free, fb_ld, fb_m, fb_e, fb_s, fb_pe, fb_add, fb_wc = (
            sem(n) for n in ("fb_free", "fb_ld", "fb_m", "fb_e", "fb_s", "fb_pe", "fb_add", "fb_wc"))
        s_third = [sem(f"s_third{i}") for i in range(NXC)]
        s_cl = [sem(f"s_cl{i}") for i in range(2)]
        s_pl = [sem(f"s_pl{i}") for i in range(2)]
        s_n00 = sem("s_n00")
        s_n0 = sem("s_n0")
        s_n1 = sem("s_n1")
        s_n1s = sem("s_n1s")
        s_bst = sem("s_bst")
        s_v2, s_sd2, s_c2 = sem("s_v2"), sem("s_sd2"), sem("s_c2")
        s_oadd = sem("s_oadd")
        s_odd = sem("s_odd")
        s_oterm, s_bias = sem("s_oterm"), sem("s_bias")
        s_oddm = sem("s_oddm")
        s_oddr = sem("s_oddr")
        s_r2 = sem("s_r2")
        s_n2 = sem("s_n2")
        s_xn = [sem(f"s_xn{i}") for i in range(NODE_SLOTS)]
        s_o = sem("s_o")
        s_out = [sem(f"s_out{i}") for i in range(NODE_SLOTS)]

        block = ctx.enter_context(nc.Block())

        def row_tiles_dma(eng, dram, sbuf, b, to_sbuf, done):
            n = block_nodes(b)
            full = n // P
            parts = []
            if full:
                parts.append((dram[b * BN_:b * BN_ + full * P, :].rearrange("(t p) f -> p t f", p=P), sbuf[:, 0:full, :]))
            if n % P:
                parts.append((dram[b * BN_ + full * P:b * BN_ + n, :], sbuf[0:n % P, full, :]))
            for d, s in parts:
                eng.dma_start(s if to_sbuf else d, d if to_sbuf else s).then_inc(done, 16)
            return len(parts)

        def row_parts(b):
            n = block_nodes(b)
            return (1 if n // P else 0) + (1 if n % P else 0)

        def space_of_windows_free(eng):
            eng.wait_ge(s_job, len(JOBS))
            for q in (KC * NB - 2, KC * NB - 1):
                eng.wait_ge(s_jobw[q % 2], 16 * (q // 2 + 1))

        def full_and_rest(b):
            tl = tiles_of(b)
            full = sum(1 for q in tl if q[2] == P)
            return ([(0, full, P)] if full else []) + [(q[0], 1, q[2]) for q in tl if q[2] < P]

        def slot_count(b, per, slots=2):
            return 16 * sum(per(i) for i in range(b % slots, b + 1, slots))

        def table_written(eng):
            for b in range(max(0, NB - ROW_SLOTS), NB):
                eng.wait_ge(s_p1w[b % ROW_SLOTS], slot_count(b, row_parts, ROW_SLOTS))

        x_parts = [sum(row_parts(b) for b in range(c * XL, min(NB, c * XL + XL))) for c in range(NXL)]
        W1_LOADS, W_LOADS, COLUMN_LOADS = 5, 7, 8

        @block.sync
        def _(sp):
            for c in range(NXL):
                for b in range(c * XL, min(NB, c * XL + XL)):
                    row_tiles_dma(sp, x, x_all[:, 4 * b:4 * b + 4, :], b, True, s_x[c])
                if c == 0:
                    for d, s in [(b1_bc[:, :], b1.partition_broadcast(P)), (W1b_bc[:, :], W1[NF, :].partition_broadcast(P)),
                                 (g1_bc[:, :], g1.partition_broadcast(P)), (W1a[:, :], W1[0:NF, :]),
                                 (W1c[:, :], W1[NF + 1:, :])]:
                        sp.dma_start(d, s).then_inc(s_w1, 16)
            for d, s in [(be1_bc[:, :], be1.partition_broadcast(P)),
                         (W2s[:, 0, :], W2[0:NF, :]), (W2s[:, 1, :], W2[NF + 1:NF + 1 + P, :]),
                         (W2s[:, 2, :], W2[NF + 1 + P:, :]),
                         (W3s[:, :, :], W3[0:KC * P, :].rearrange("(c p) f -> p c f", p=P)),
                         (W3o_bc[:, :], W3[KC * P, :].partition_broadcast(P)), (b3_bc[:, :], b3.partition_broadcast(P))]:
                sp.dma_start(d, s).then_inc(s_w, 16)
            def load_indices():
                sp.wait_ge(s_ei0, 3)
                sp.dma_start(idx[:, 0:TCOLS - 1], src_main).then_inc(s_ei, 16)
                sp.dma_start(idx[0:TAIL, TCOLS - 1:], src_tail).then_inc(s_ei, 16)
                sp.dma_start(dst_hi_i[:, 0:TCOLS - 1], dst_main).then_inc(s_ei, 16)
                sp.dma_start(dst_hi_i[0:TAIL, TCOLS - 1:], dst_tail).then_inc(s_ei, 16)
                for c in range(GC):
                    n = min(P, GF - c * P)
                    sp.dma_start(grp_i[0:n, c, :], dst[c * GE * P:(c * P + n) * GE].rearrange("(g e) -> g e", e=GE)).then_inc(s_grp, 16)
                sp.dma_start(grp_i[GF % P:GF % P + 1, GF // P, :], dst[E - GE:E].rearrange("(g e) -> g e", g=1)).then_inc(s_grp, 16)

            def load_ea(u):
                if u >= EA_SLOTS:
                    sp.wait_ge(s_eam, EA_GROUPS * (u - EA_SLOTS + 1))
                a = u * EA_GROUPS * GE
                n = min(EA_GROUPS * GE, E - a)
                sp.dma_start(ea_s[u % EA_SLOTS][:, 0:n], eaT[:, a:a + n]).then_inc(s_ea[u % EA_SLOTS], 16)
            for b in range(NB):
                sp.wait_ge(s_p1, b + 1)
                row_tiles_dma(sp, P1_d, p1_s[b % ROW_SLOTS], b, False, s_p1w[b % ROW_SLOTS])
                if b == 0:
                    load_indices()
                for u in range(min(EA_SLOTS, EAU)):
                    if b == min(XL + u, NB - 1):
                        load_ea(u)

            def store_part(j):
                b, c = JOBS[j]
                if c == KC:
                    return
                n, q = block_nodes(b), KC * b + c
                sp.wait_ge(s_jobs, j + 1)
                sp.dma_start(early_d[c, :, b * BN_:b * BN_ + n], part_s[q % 2][:, 0:n]).then_inc(s_jobw[q % 2], 16)

            for g in range(NG):
                u = g // EA_GROUPS + 1
                if g % EA_GROUPS == EA_GROUPS - 1 and u + EA_SLOTS - 1 < EAU:
                    load_ea(u + EA_SLOTS - 1)
                sp.wait_ge(s_m, g + 1)
                r, w = rows(g), tiles(g) * L
                sp.dma_start(m_d[g, 0:r, 0:w], m_s[g % M_SLOTS][0:r, 0:w]).then_inc(s_mw[g % M_SLOTS], 16)
                if g == SEND:
                    sp.wait_ge(s_rngs, 1)
                    sp.dma_start(range_d, rngT[:, :]).then_inc(s_rngw, 16)
                if g == SEND + 2:
                    sp.wait_ge(s_rngw, 16)
                    sp.dma_start(base_bc[:, :], range_d[0:GC, :].rearrange("c p -> (c p)").partition_broadcast(P)).then_inc(s_rngl, 16)
                    sp.dma_start(rng_row[:, :], range_d.rearrange("(a c) p -> a (c p)", a=1)).then_inc(s_rngl, 16)
                if g - 1 in job_of:
                    store_part(job_of[g - 1])
            for s in range(M_SLOTS):
                sp.wait_ge(s_mw[s], 16 * len(range(s, NG, M_SLOTS)))
            sp.wait_ge(s_st, NG)
            sp.wait_ge(s_q, NG)
            sp.wait_ge(s_flag, 1)
            flag = sp.alloc_register("wide_sp")
            sp.load(flag, wide_i[0:1, 0:1])
            with sp.If_eq(flag, 0):
                for g in range(NG):
                    if g >= M_SLOTS:
                        sp.wait_ge(s_seg, g - M_SLOTS + 1)
                    r, w = rows(g), tiles(g) * L
                    sp.dma_start(m_s[g % M_SLOTS][0:r, 0:w], m_d[g, 0:r, 0:w]).then_inc(s_ml[g % M_SLOTS], 16)
            with sp.Else():
                with sp.Fori(0, GF) as g:
                    sp.wait_ge(fb_free, g + 1)
                    sp.dma_start(m_s[0], m_d[bass.ds(g, 1), :, :].rearrange("g p w -> p (g w)")).then_inc(fb_ld, 16)
                sp.wait_ge(fb_free, GF + 1)
                sp.dma_start(m_s[0][0:TAIL, 0:L], m_d[GF, 0:TAIL, 0:L]).then_inc(fb_ld, 16)

            sp.wait_ge(s_cntw, 16)
            flat_cnt = cnt_d.rearrange("a h p -> a (h p)")

            def load_counts(b):
                n, c0 = block_nodes(b), b * BN_
                for a, d in ((0, cnt_bc), (1, inv_bc)):
                    sp.dma_start(d[b % 2][:, 0:n], flat_cnt[a, c0:c0 + n].partition_broadcast(P)).then_inc(s_cl[b % 2], 16)

            def load_third_plane(b):
                c0, z = b * BN_, min(N, (b + XC) * BN_)
                sp.dma_start(area[:, c0:z], early_d[2, :, c0:z]).then_inc(s_third[b // XC], 16)

            load_counts(0)
            sp.wait_ge(s_B, 1)
            for q in (KC * NB - 2, KC * NB - 1):
                sp.wait_ge(s_jobw[q % 2], 16 * (q // 2 + 1))
            load_counts(1)
            for b in range(NB):
                n, c0 = block_nodes(b), b * BN_
                if b >= 2:
                    sp.wait_ge(s_n1s, b - 1)
                sp.dma_start(part[b % 2][:, :, 0:n], early_d[0:2, :, c0:c0 + n].rearrange("c p n -> p c n")).then_inc(s_pl[b % 2], 16)
                if b + 2 < NB:
                    sp.wait_ge(s_n0, b + 1)
                    load_counts(b + 2)
                if b % XC == 0:
                    for first in ([0] if b == 0 else []) + ([b + XC] if b + XC < NB else []):
                        load_third_plane(first)
            sp.wait_ge(s_n0, NB)
            sp.wait_ge(s_n1s, NB)
            for b in range(NB):
                i = b % NODE_SLOTS
                if b >= NODE_SLOTS:
                    sp.wait_ge(s_o, b - NODE_SLOTS + 1)
                row_tiles_dma(sp, x, x_n[i], b, True, s_xn[i])

        @block.gpsimd
        def _(pool):
            pool.memset(idx[:, TCOLS - 1:], 0).then_inc(s_ei0, 1)
            pool.memset(dst_hi_i[:, TCOLS - 1:], 0).then_inc(s_ei0, 1)
            pool.memset(grp_i, 0).then_inc(s_ei0, 1)
            pool.memset(ident[:, :], 0.0).then_inc(s_const, 1)
            pool.iota(iota[:, :], pattern=[[1, P]], base=0, channel_multiplier=0,
                      allow_small_or_imprecise_dtypes=True).then_inc(s_const, 1)
            pool.iota(iota_b[:, :], pattern=[[1, P]], base=0, channel_multiplier=0,
                      allow_small_or_imprecise_dtypes=True).then_inc(s_const, 1)
            pool.memset(ones[:, :], 1.0).then_inc(s_const, 1)
            pool.memset(eps[:, :], EPS).then_inc(s_const, 1)
            pool.memset(bcol[:, :], 0.0).then_inc(s_const, 1)
            pool.wait_ge(s_const, 6)
            pool.affine_select(out=ident[:, :], in_=ident[:, :], compare_op=ALU.not_equal, fill=1.0, base=0,
                               pattern=[[-1, P]], channel_multiplier=1).then_inc(s_const, 1)
            with nc.allow_non_contiguous_dma(reason="a few hundred parameters, once"):
                for v, c in ((g2, g2c), (be2, be2c), (b2, b2c), (W2[NF, :], W2bc)):
                    pool.dma_start(c[:, 0:KC], v[0:KC * P].rearrange("(c p) -> p c", p=P)).then_inc(s_wp, 16)
                    pool.dma_start(c[:, KC:], v[KC * P:].partition_broadcast(P)).then_inc(s_wp, 16)
            pool.wait_ge(s_ei, 64)
            table_written(pool)
            for g in range(NG):
                s, r = g % M_SLOTS, rows(g)
                if g >= M_SLOTS:
                    pool.wait_ge(s_mw[s], 16 * (g // M_SLOTS))
                    pool.wait_ge(s_pm, g - M_SLOTS + 1)
                    pool.wait_ge(s_q, g - M_SLOTS + 1)
                for k in range(tiles(g)):
                    pool.indirect_dma_start(
                        out=m_s[s][0:r, k * L:(k + 1) * L], out_offset=None, in_=P1_d,
                        in_offset=bass.IndirectOffsetOnAxis(ap=idx[0:r, GT * g + k:GT * g + k + 1].bitcast(U32), axis=0),
                    ).then_inc(s_gat[s][k], 16)
            pool.wait_ge(s_cnts, 1)
            pool.dma_start(cnt_d.rearrange("a h p -> h a p"), cnt_s[:, :, :]).then_inc(s_cntw, 16)
            for b in range(NB):
                n, c0 = block_nodes(b), b * BN_
                pool.wait_ge(s_n00, b + 1)
                v = sums[:, :, c0:c0 + n]
                pool.tensor_tensor(v, v, inv_bc[b % 2][:, 0:n].unsqueeze(1).to_broadcast([P, 2, n]), ALU.mult).then_inc(s_n0, 1)
            for b in range(NB):
                pool.wait_ge(s_o, b + 1)
                row_tiles_dma(pool, out, o_n[b % NODE_SLOTS], b, False, s_out[b % NODE_SLOTS])
            for b in range(max(0, NB - NODE_SLOTS), NB):
                pool.wait_ge(s_out[b % NODE_SLOTS], slot_count(b, row_parts, NODE_SLOTS))

        @block.scalar
        def _(act):
            act.wait_ge(s_const, 7)

            def chunk_tiles(c):
                return 4 * XL * c, min(4 * NB, 4 * XL * (c + 1))

            def ln_sqrt(c):
                a, z = chunk_tiles(c)
                act.wait_ge(s_lnmv, c + 1)
                act.activation(ln_r[:, a:z], ln_mv[:, a:z, 1], ACT.Sqrt, bias=eps[:, 0:1]).then_inc(s_lnsd, 1)

            def h_rows(b):
                if b >= ROW_SLOTS:
                    act.wait_ge(s_hT, b - ROW_SLOTS + 1)
                for t, a, r in tiles_of(b):
                    i = 4 * b + t
                    ins = act.activation(h_row[b % ROW_SLOTS][0:r, t, :], x_all[0:r, i, :], ACT.Relu,
                                         bias=ln_b[0:r, i:i + 1], scale=ln_r[0:r, i:i + 1])
                ins.then_inc(s_h, 1)

            def hT_copy(b):
                n = block_nodes(b)
                act.wait_ge(s_hT, b + 1)
                act.activation(hT[b][:, 0:n], psum[:, 6 + b % 2, 0:n], ACT.Copy).then_inc(s_hTs, 1)

            for c in range(min(2, NXL)):
                ln_sqrt(c)
            for b in range(NB):
                c = b // XL
                if b % XL == 0:
                    act.wait_ge(s_lnr, c + 1)
                h_rows(b)
                if b >= 1:
                    hT_copy(b - 1)
                if b % XL == XL - 1 and c + 2 < NXL:
                    ln_sqrt(c + 2)
            hT_copy(NB - 1)
            for g in range(NG):
                r, w = rows(g), tiles(g) * L
                act.wait_ge(s_m, g + 1)
                if g >= 2:
                    act.wait_ge(s_st, g - 1)
                act.activation(q_s[g % 2][0:r, 0:w], m_s[g % M_SLOTS][0:r, 0:w], ACT.Square).then_inc(s_q, 1)
                if g in job_of:
                    j = job_of[g]
                    b, c = JOBS[j]
                    act.wait_ge(s_job, j + 1)
                    if c < KC:
                        n, q = block_nodes(b), KC * b + c
                        if q >= 2:
                            act.wait_ge(s_jobw[q % 2], 16 * (q // 2))
                        act.activation(part_s[q % 2][:, 0:n], ps_job[:, 0:n], ACT.Identity,
                                       bias=b2c[:, c:c + 1]).then_inc(s_jobs, 1)
                    else:
                        for t0, m, r in full_and_rest(b):
                            ins = act.activation(odd[0:r, 4 * b + t0:4 * b + t0 + m], ps_job[0:r, t0:t0 + m],
                                                 ACT.Identity, bias=b2c[0:r, KC:])
                        ins.then_inc(s_jobs, 1)
            act.wait_ge(s_var, 1)
            act.activation(bn_row[:, SD, :], bn_row[:, VAR, :], ACT.Sqrt, bias=eps[:, 0:1]).then_inc(s_sd, 1)
            space_of_windows_free(act)
            flag = act.alloc_register("wide_act")
            act.wait_ge(s_flag, 1)
            act.load(flag, wide_i[0:1, 0:1])
            with act.If_eq(flag, 0):
                for g in range(NG):
                    r, nt = rows(g), tiles(g)
                    if g >= 2:
                        act.wait_ge(s_sel, g - 1)
                    for k in range(max(1, nt - 1)):
                        ins = act.activation(dist[0:r, g % 2, k, :], iota[0:r, 0:WIN], ACT.Abs,
                                             bias=dst_f[0:r, GT * g + k:GT * g + k + 1])
                    ins.then_inc(s_dist, 1)
                    act.wait_ge(s_dist, g + 1)
                    if g >= 4:
                        act.wait_ge(s_seg, g - 3)
                    na = max(1, nt - 1)
                    act.activation(sel[0:r, g % 4, 0:na, :], dist[0:r, g % 2, 0:na, :], ACT.Relu,
                                   bias=ones[0:r, 0:1], scale=-1.0).then_inc(s_sel, 1)
            with act.Else():
                pass
            act.wait_ge(s_v2, 1)
            act.activation(bn2[:, 0, :], bn2_mv[:, :, 1], ACT.Sqrt, bias=eps[:, 0:1]).then_inc(s_sd2, 1)
            act.wait_ge(s_c2, 1)
            for b in range(NB):
                n, c0 = block_nodes(b), b * BN_
                for c in range(KC):
                    ins = act.activation(plane[c][:, c0:c0 + n], plane[c][:, c0:c0 + n], ACT.Relu,
                                         bias=bn2[:, 3, c:c + 1], scale=bn2[:, 2, c:c + 1])
                ins.then_inc(s_r2, 1)
                if b == 0:
                    act.activation(odd[:, :], odd[:, :], ACT.Relu,
                                   bias=bn2[:, 3, KC:], scale=bn2[:, 2, KC:]).then_inc(s_oddr, 1)

        @block.vector
        def _(dve):
            steps = [0]

            def step(ins):
                steps[0] += 1
                ins.then_inc(s_v, 1)
                dve.wait_ge(s_v, steps[0])

            dve.wait_ge(s_const, 7)

            def ln_stats(c):
                lo, hi = c * XL, min(NB, c * XL + XL)
                dve.wait_ge(s_x[c], 16 * x_parts[c])
                tl = [(4 * b + t, r) for b in range(lo, hi) for t, _, r in tiles_of(b)]
                for i, r in tl:
                    ins = dve.bn_stats(ln_st[0:r, i, :], x_all[0:r, i, :])
                step(ins)
                for i, r in tl:
                    ins = dve.bn_aggr(ln_mv[0:r, i, :], ln_st[0:r, i, :])
                ins.then_inc(s_lnmv, 1)

            def ln_scale(c):
                a, z = 4 * XL * c, min(4 * NB, 4 * XL * (c + 1))
                dve.wait_ge(s_lnsd, c + 1)
                step(dve.reciprocal(ln_r[:, a:z], ln_r[:, a:z]))
                dve.scalar_tensor_tensor(ln_b[:, a:z], ln_mv[:, a:z, 0], -1.0, ln_r[:, a:z],
                                         ALU.mult, ALU.mult).then_inc(s_lnr, 1)

            dve.memset(ln_mv[:, :, :], 0.0)
            step(dve.memset(odd[:, :], 0.0))
            ln_stats(0)
            dve.wait_ge(s_w1, 16 * W1_LOADS)
            step(dve.tensor_scalar(sgn[:, :], g1_bc[:, :], 0.0, 2.0, ALU.is_ge, ALU.mult))
            step(dve.tensor_scalar(sgn[:, :], sgn[:, :], -1.0, None, ALU.add))
            dve.tensor_tensor(g1_bc[:, :], g1_bc[:, :], sgn[:, :], ALU.mult)
            step(dve.scalar_tensor_tensor(b1_bc[:, :], W1b_bc[:, :], bcol[:, 0:1], b1_bc[:, :], ALU.mult, ALU.add))
            dve.tensor_tensor(b1_bc[:, :], b1_bc[:, :], sgn[:, :], ALU.mult)
            dve.tensor_tensor(W1a[:, :], W1a[:, :], sgn[:, :], ALU.mult)
            dve.tensor_tensor(W1c[:, :], W1c[:, :], sgn[0:EF, :], ALU.mult).then_inc(s_sgn, 1)

            def table_rows(b):
                dve.wait_ge(s_p1m, b + 1)
                if b >= ROW_SLOTS:
                    dve.wait_ge(s_p1w[b % ROW_SLOTS], slot_count(b - ROW_SLOTS, row_parts, ROW_SLOTS))
                for t, _, r in tiles_of(b):
                    if t % 2 == 0:
                        n2 = min(2, len(tiles_of(b)) - t)
                        if all(q[2] == P for q in tiles_of(b)[t:t + n2]):
                            parts = [(t, n2, P)]
                        else:
                            parts = [(q[0], 1, q[2]) for q in tiles_of(b)[t:t + n2]]
                        for t0, m, rr in parts:
                            ins = dve.tensor_tensor(
                                p1_s[b % ROW_SLOTS][0:rr, t0:t0 + m, :],
                                ps_m[b % 2][0:rr, t0 * L:(t0 + m) * L].rearrange("p (t f) -> p t f", f=L),
                                b1_bc[0:rr, :].unsqueeze(1).to_broadcast([rr, m, L]), ALU.add)
                ins.then_inc(s_p1, 1)

            def split_destinations():
                dve.wait_ge(s_ei, 64)
                dve.tensor_copy(dst_f[:, :], dst_hi_i[:, :])
                step(dve.tensor_scalar(dst_lo_i[:, :], dst_hi_i[:, :], P - 1, None, ALU.bitwise_and))
                step(dve.tensor_scalar(dst_hi_i[:, :], dst_hi_i[:, :], P.bit_length() - 1, None,
                                       ALU.logical_shift_right))
                dve.tensor_copy(dst_hi, dst_hi_i[:, :])
                step(dve.tensor_copy(dst_lo, dst_lo_i[:, :]))

            def group_destinations():
                dve.wait_ge(s_grp, 16 * (GC + 1))
                step(dve.tensor_copy(grp_f, grp_i))

            def group_range():
                step(dve.tensor_reduce(rng[:, 0:GC], grp_f, AX.X, ALU.min))
                step(dve.tensor_reduce(rng[:, GC:], grp_f, AX.X, ALU.max))
                dve.tensor_tensor(rng[:, GC:], rng[:, GC:], rng[:, 0:GC], ALU.subtract).then_inc(s_rng, 1)

            def node_bias():
                dve.wait_ge(s_w, 16 * W_LOADS)
                dve.wait_ge(s_wp, 16 * COLUMN_LOADS)
                dve.scalar_tensor_tensor(b2c[:, :], W2bc[:, :], bcol[:, 0:1], b2c[:, :], ALU.mult, ALU.add).then_inc(s_sgn, 1)

            ln_scale(0)
            for c in range(1, min(4, NXL)):
                ln_stats(c)
                if c == 1:
                    ln_scale(c)
            beside = [node_bias, split_destinations]
            for b in range(NB):
                c = b // XL
                table_rows(b)
                if b % XL == XL - 1:
                    if c + 2 < NXL:
                        ln_scale(c + 2)
                    if c + 4 < NXL:
                        ln_stats(c + 4)
                elif c >= 1 and beside:
                    beside.pop(0)()
            for piece in beside:
                piece()

            def turned_ranges():
                dve.wait_ge(s_rngT, 1)
                dve.tensor_copy(rngT[:, :], psum[0:2 * GC, 7, 0:P]).then_inc(s_rngs, 1)

            def windows_of_groups():
                dve.wait_ge(s_rngl, 32)
                dve.tensor_copy(base_i[:, :], rng_row[:, 0:GC * P])
                step(dve.tensor_reduce(wide[:, :], rng_row[:, GC * P:], AX.X, ALU.max))
                step(dve.tensor_scalar(wide[:, :], wide[:, :], float(WIN), None, ALU.is_ge))
                dve.tensor_copy(wide_i[:, :], wide[:, :])
                dve.tensor_tensor(dst_f[:, TCOLS - 1:], base_bc[:, GF:GF + 1], dst_f[:, TCOLS - 1:], ALU.subtract)
                main = dst_f[:, 0:GF * GT].rearrange("p (g k) -> p g k", k=GT)
                dve.tensor_tensor(main, base_bc[:, 0:GF].unsqueeze(2).to_broadcast([P, GF, GT]), main,
                                  ALU.subtract).then_inc(s_flag, 1)

            ranges = {RANGE: group_destinations, RANGE + 1: group_range, TURN + 1: turned_ranges,
                      BACK: windows_of_groups}
            def one_hot(g):
                if g >= 2:
                    dve.wait_ge(s_cnt, g - 1)
                r = rows(g)
                for k in range(tiles(g)):
                    j = GT * g + k
                    dve.tensor_scalar(hot_hi[0:r, g % 2, k, 0:NH], iota_b[0:r, 0:NH], dst_hi[0:r, j:j + 1], None, ALU.is_equal)
                    ins = dve.tensor_scalar(hot_lo[0:r, g % 2, k, :], iota_b[0:r, :], dst_lo[0:r, j:j + 1], None, ALU.is_equal)
                ins.then_inc(s_hot, 1)

            one_hot(0)
            zero_at = NB * BN_
            zero_block = {job_group[(KC + 1) * (b + 1) - 1] + 1: b for b in range(NB)}
            H2 = 2 * L
            for g in range(NG):
                s, r, w = g % M_SLOTS, rows(g), tiles(g) * L
                if g > BACK and zero_at < 2 * NPAD:
                    z = min(2 * NPAD, zero_at + ZERO_COLS)
                    dve.memset(flat[:, zero_at:z], 0.0)
                    zero_at = z
                if g in zero_block:
                    b = zero_block[g]
                    dve.wait_ge(s_job, (KC + 1) * (b + 1))
                    dve.memset(hT[b], 0.0)
                if g >= 1:
                    dve.wait_ge(s_q, g)
                    q = q_s[(g - 1) % 2]
                    dve.tensor_tensor(q[:, 0:H2], q[:, 0:H2], q[:, H2:2 * H2], ALU.add).then_inc(s_pq, 1)
                for k in range(tiles(g)):
                    dve.wait_ge(s_gat[s][k], 16 * (g // M_SLOTS + 1))
                dve.wait_ge(s_eam, g + 1)
                dve.tensor_tensor(m_s[s][0:r, 0:w], ps_m[g % 2][0:r, 0:w], m_s[s][0:r, 0:w], ALU.add).then_inc(s_m, 1)
                if g + 1 < NG:
                    one_hot(g + 1)
                if g in ranges:
                    ranges[g]()
                if g < GF:
                    dve.wait_ge(s_m, g + 1)
                    if g >= 2:
                        dve.wait_ge(s_st, g - 1)
                    dve.tensor_tensor(m_pair[:, g % 2, :], m_s[s][:, 0:H2], m_s[s][:, H2:2 * H2], ALU.add).then_inc(s_pm, 1)
            while zero_at < 2 * NPAD:
                z = min(2 * NPAD, zero_at + ZERO_COLS)
                step(dve.memset(flat[:, zero_at:z], 0.0))
                zero_at = z
            assert all(g < NG for g in zero_block)
            dve.wait_ge(s_cnt, NG)
            step(dve.tensor_copy(cnt_s[:, 0, :], ps_cnt[0:NH, 0:P]))
            step(dve.tensor_scalar(cnt_s[:, 1, :], cnt_s[:, 0, :], 1.0, None, ALU.max))
            dve.reciprocal(cnt_s[:, 1, :], cnt_s[:, 1, :]).then_inc(s_cnts, 1)
            dve.wait_ge(s_st, NG)
            for ps, row in ((ps_sum, MEAN), (ps_sq, EX2)):
                step(dve.tensor_scalar(bn_row[:, row, :], ps[:, 0:L], 1.0 / E, None, ALU.mult))
                step(dve.scalar_tensor_tensor(bn_row[:, row, :], ps[:, L:2 * L], 1.0 / E, bn_row[:, row, :],
                                              ALU.mult, ALU.add))
            step(dve.tensor_tensor(bn_row[:, VAR, :], bn_row[:, MEAN, :], bn_row[:, MEAN, :], ALU.mult))
            step(dve.tensor_tensor(bn_row[:, VAR, :], bn_row[:, EX2, :], bn_row[:, VAR, :], ALU.subtract))
            dve.tensor_scalar(bn_row[:, VAR, :], bn_row[:, VAR, :], 0.0, None, ALU.max).then_inc(s_var, 1)
            dve.wait_ge(s_sd, 1)
            step(dve.reciprocal(bn_row[:, RS, :], bn_row[:, SD, :]))
            step(dve.tensor_tensor(bn_row[:, A, :], g1_bc[:, :], bn_row[:, RS, :], ALU.mult))
            step(dve.tensor_tensor(bn_row[:, C, :], bn_row[:, A, :], bn_row[:, MEAN, :], ALU.mult))
            step(dve.tensor_tensor(bn_row[:, C, :], be1_bc[:, :], bn_row[:, C, :], ALU.subtract))
            step(dve.tensor_scalar(bn_row[:, A, :], bn_row[:, A, :], SMALLEST, None, ALU.max))
            step(dve.reciprocal(bn_row[:, INV, :], bn_row[:, A, :]))
            dve.tensor_tensor(bn_row[:, NEGT, :], bn_row[:, C, :], bn_row[:, INV, :], ALU.mult).then_inc(s_row, 1)
            dve.wait_ge(s_row, 1)
            step(dve.tensor_scalar(T[:, :], bn_row[:, NEGT, :], -1.0, None, ALU.mult))

            space_of_windows_free(dve)
            flag = dve.alloc_register("wide_dve")
            dve.load(flag, wide_i[0:1, 0:1])

            def clip(r, nt, slot):
                v = m_s[slot][0:r, 0:nt * L].rearrange("p (k f) -> p k f", f=L)
                return dve.tensor_tensor(v, v, T[0:r, :].unsqueeze(1).to_broadcast([r, nt, L]), ALU.max)

            with dve.If_eq(flag, 0):
                def add_window(g):
                    at = dve.value_load(base_i[0:1, g:g + 1], min_val=0, max_val=N - 1)
                    dve.wait_ge(s_seg, g + 1)
                    if g:
                        dve.wait_ge(s_add, g)
                    win = sums[:, :, bass.ds(at, WIN)]
                    dve.tensor_tensor(win, win, ps_seg[g % 3].rearrange("p (h w) -> p h w", h=2),
                                      ALU.add).then_inc(s_add, 1)
                for g in range(NG):
                    s = g % M_SLOTS
                    if g < GF:
                        if g >= 4:
                            dve.wait_ge(s_seg, g - 3)
                        dve.tensor_scalar(sel[:, g % 4, GT - 1, :], iota[:, :], dst_f[:, GT * g + GT - 1:GT * g + GT],
                                          0.0, ALU.add, ALU.is_equal)
                    dve.wait_ge(s_ml[s], 16 * (g // M_SLOTS + 1))
                    clip(rows(g), tiles(g), s).then_inc(s_r, 1)
                    if g >= 2:
                        add_window(g - 2)
                add_window(NG - 2)
                add_window(NG - 1)
                dve.wait_ge(s_add, NG)
                dve.memset(fb_t[:, :], 0.0).then_inc(s_B, 1)
            with dve.Else():
                def group(g, r, nt, first):
                    dve.wait_ge(fb_ld, (g + 1) * 16)
                    clip(r, nt, 0).then_inc(fb_m, 1)
                    if first is None:
                        dve.tensor_copy(fb_hi[0:r, 0:nt], dst_hi[0:r, TCOLS - 1:]).then_inc(fb_m, 1)
                        dve.tensor_copy(fb_lo[0:r, 0:nt], dst_lo[0:r, TCOLS - 1:]).then_inc(fb_m, 1)
                    else:
                        dve.tensor_copy(fb_hi[:, :], dst_hi[:, bass.ds(g * GT, GT)]).then_inc(fb_m, 1)
                        dve.tensor_copy(fb_lo[:, :], dst_lo[:, bass.ds(g * GT, GT)]).then_inc(fb_m, 1)
                    dve.memset(fb_w[:, :], 0.0).then_inc(fb_m, 1)
                    dve.wait_ge(fb_m, (g + 1) * 4)
                    dve.tensor_copy(fb_t[:, :], fb_w[:, :])
                    with dve.Fori(0, NH) as w:
                        i = g * NH + w
                        dve.tensor_scalar(fb_eq[0:r, 0:nt], fb_hi[0:r, 0:nt], fb_w[0:r, 0:1], None,
                                          ALU.is_equal).then_inc(fb_e, 1)
                        dve.wait_ge(fb_e, i + 1)
                        for k in range(nt):
                            ins = dve.tensor_scalar(fb_sel[0:r, k, :], iota[0:r, :], fb_lo[0:r, k:k + 1],
                                                    fb_eq[0:r, k:k + 1], ALU.is_equal, ALU.mult)
                        ins.then_inc(fb_s, 1)
                        dve.tensor_scalar(fb_w[:, :], fb_w[:, :], 1.0, None, ALU.add).then_inc(fb_wc, 1)
                        dve.wait_ge(fb_wc, i + 1)
                        dve.wait_ge(fb_pe, i + 1)
                        win = sums[:, :, bass.ds(w * P, P)]
                        dve.tensor_tensor(win, win, psum[:, 0, 0:2 * P].rearrange("p (h w) -> p h w", h=2),
                                          ALU.add).then_inc(fb_add, 1)
                        dve.wait_ge(fb_add, i + 1)
                    dve.memset(fb_t[:, :], 0.0).then_inc(fb_free, 1)
                dve.memset(fb_t[:, :], 0.0).then_inc(fb_free, 1)
                with dve.Fori(0, GF) as g:
                    group(g, P, GT, 0)
                group(GF, TAIL, 1, None)
                dve.wait_ge(fb_free, GF + 2)
                dve.memset(fb_t[:, :], 0.0).then_inc(s_B, 1)

            dve.wait_ge(s_col, 1)
            cols = ps_col.rearrange("p (v f) -> p v f", f=P)[:, :, 0]
            dve.tensor_copy(a_col[:, :], cols[:, 0:2])
            step(dve.tensor_copy(negt_col[:, :], cols[:, 2:4]))
            for h in range(2):
                step(dve.tensor_scalar(W2s[:, 1 + h, :], W2s[:, 1 + h, :], a_col[:, h:h + 1], None, ALU.mult))

            def centre(b):
                n, c0 = block_nodes(b), b * BN_
                dve.wait_ge(s_cl[b % 2], 32 * (b // 2 + 1))
                for h in range(2):
                    v = sums[:, h, c0:c0 + n]
                    ins = dve.scalar_tensor_tensor(v, cnt_bc[b % 2][:, 0:n], negt_col[:, h:h + 1], v, ALU.mult, ALU.add)
                ins.then_inc(s_n00, 1)

            def pre(b):
                n, c0, bank = block_nodes(b), b * BN_, 4 * (b % 2)
                dve.wait_ge(s_n1, b + 1)
                dve.wait_ge(s_third[b // XC], 16)
                dve.wait_ge(s_pl[b % 2], 16 * (b // 2 + 1))
                for t0, m, r in full_and_rest(b):
                    v = odd[0:r, 4 * b + t0:4 * b + t0 + m]
                    dve.tensor_tensor(v, v, psum[0:r, bank + KC, t0:t0 + m], ALU.add).then_inc(s_oadd, 1)
                for c, early in enumerate((part[b % 2][:, 0, 0:n], part[b % 2][:, 1, 0:n], area[:, c0:c0 + n])):
                    ins = dve.tensor_tensor(plane[c][:, c0:c0 + n], psum[:, bank + c, 0:n], early, ALU.add)
                ins.then_inc(s_n1s, 1)

            def statistics(b):
                n, c0 = block_nodes(b), b * BN_
                dve.wait_ge(s_n1s, b + 1)
                for c in range(KC):
                    ins = dve.bn_stats(bn2_st[:, c, b, :], plane[c][:, c0:c0 + n])
                ins.then_inc(s_bst, 1)

            def odd_sums():
                dve.wait_ge(s_oadd, sum(len(full_and_rest(b)) for b in range(NB)))
                step(dve.tensor_tensor(odd_sq[:, :], odd[:, :], odd[:, :], ALU.mult))
                dve.tensor_reduce(odd_sum[:, 0:1], odd[:, :], AX.X, ALU.add)
                dve.tensor_reduce(odd_sum[:, 1:2], odd_sq[:, :], AX.X, ALU.add).then_inc(s_odd, 1)

            dve.wait_ge(s_B, 1)
            centre(0)
            centre(1)
            for b in range(NB):
                pre(b)
                if b + 2 < NB:
                    centre(b + 2)
                if b == NB - 1:
                    odd_sums()
                statistics(b)
            dve.wait_ge(s_bst, NB)
            for c in range(KC):
                dve.bn_aggr(bn2_mv[:, c, :], bn2_st[:, c, :, :].rearrange("p b s -> p (b s)"))
            dve.wait_ge(s_oddm, 1)
            step(dve.tensor_scalar(odd_sum[:, 2:4], psum[:, ODD_BANK, 0:2], 1.0 / N, None, ALU.mult))
            dve.tensor_copy(bn2_mv[:, KC, 0:1], odd_sum[:, 2:3])
            step(dve.tensor_tensor(odd_sum[:, 2:3], odd_sum[:, 2:3], odd_sum[:, 2:3], ALU.mult))
            step(dve.tensor_tensor(odd_sum[:, 3:4], odd_sum[:, 3:4], odd_sum[:, 2:3], ALU.subtract))
            dve.tensor_scalar(bn2_mv[:, KC, 1:2], odd_sum[:, 3:4], 0.0, None, ALU.max).then_inc(s_v2, 1)
            dve.wait_ge(s_sd2, 1)
            step(dve.reciprocal(bn2[:, 1, :], bn2[:, 0, :]))
            step(dve.tensor_tensor(bn2[:, 2, :], g2c[:, :], bn2[:, 1, :], ALU.mult))
            step(dve.tensor_tensor(bn2[:, 3, :], bn2[:, 2, :], bn2_mv[:, :, 0], ALU.mult))
            dve.tensor_tensor(bn2[:, 3, :], be2c[:, :], bn2[:, 3, :], ALU.subtract).then_inc(s_c2, 1)
            dve.wait_ge(s_oddr, 1)
            for b in range(NB):
                i = b % NODE_SLOTS
                dve.wait_ge(s_n2, b + 1)
                if b >= NODE_SLOTS:
                    dve.wait_ge(s_out[i], slot_count(b - NODE_SLOTS, row_parts, NODE_SLOTS))
                for t, _, r in tiles_of(b):
                    ins = dve.scalar_tensor_tensor(o_n[i][0:r, t, :], W3o_bc[0:r, :], odd[0:r, 4 * b + t:4 * b + t + 1],
                                                   psum[0:r, b % 4, t * P:(t + 1) * P], ALU.mult, ALU.add)
                ins.then_inc(s_oterm, 1)
                dve.wait_ge(s_oterm, b + 1)
                for t0, m, r in full_and_rest(b):
                    v = o_n[i][0:r, t0:t0 + m, :]
                    ins = dve.tensor_tensor(v, v, b3_bc[0:r, :].unsqueeze(1).to_broadcast([r, m, NF]), ALU.add)
                ins.then_inc(s_bias, 1)
                dve.wait_ge(s_bias, b + 1)
                dve.wait_ge(s_xn[i], slot_count(b, row_parts, NODE_SLOTS))
                for t0, m, r in full_and_rest(b):
                    v = o_n[i][0:r, t0:t0 + m, :]
                    ins = dve.scalar_tensor_tensor(v, v, 0.0, x_n[i][0:r, t0:t0 + m, :], ALU.max, ALU.add)
                ins.then_inc(s_o, 1)

        @block.tensor
        def _(pe):
            pe.wait_ge(s_const, 7)
            pe.wait_ge(s_sgn, 1)

            def turn(b):
                pe.wait_ge(s_h, b + 1)
                if b >= 2:
                    pe.wait_ge(s_hTs, b - 1)
                for t, _, r in tiles_of(b):
                    ins = pe.transpose(psum[:, 6 + b % 2, t * P:t * P + r], h_row[b % ROW_SLOTS][0:r, t, :], ident[0:r, 0:r])
                ins.then_inc(s_hT, 1)

            def table(b):
                pe.wait_ge(s_hTs, b + 1)
                if b >= 2:
                    pe.wait_ge(s_p1, b - 1)
                for t, _, r in tiles_of(b):
                    ins = pe.matmul(ps_m[b % 2][0:r, t * L:(t + 1) * L], hT[b][:, t * P:t * P + r], W1a[:, :],
                                    start=True, stop=True)
                ins.then_inc(s_p1m, 1)

            for b in range(NB):
                turn(b)
                if b >= 1:
                    table(b - 1)
            table(NB - 1)
            pe.wait_ge(s_p1, NB)

            def stats(g):
                if g < GF:
                    pe.wait_ge(s_pm, g + 1)
                    pe.wait_ge(s_pq, g + 1)
                    r, w, m = P, 2 * L, m_pair[:, g % 2, :]
                else:
                    pe.wait_ge(s_q, g + 1)
                    r, w, m = TAIL, L, m_s[g % M_SLOTS]
                for ps, v in ((ps_sum, m), (ps_sq, q_s[g % 2])):
                    ins = pe.matmul(ps[:, 0:w], ones[0:r, :], v[0:r, 0:w], start=(g == 0), stop=(g == NG - 1),
                                    skip_group_check=True)
                ins.then_inc(s_st, 1)

            def early_part(j):
                b, c = JOBS[j]
                pe.wait_ge(s_jobs, j)
                pe.wait_ge(s_rngs, 1)
                if c < KC:
                    n = block_nodes(b)
                    ins = pe.matmul(ps_job[:, 0:n], W2s[:, 0, c * P:(c + 1) * P], hT[b][:, 0:n], start=True, stop=True)
                else:
                    for t, _, r in tiles_of(b):
                        ins = pe.matmul(ps_job[0:r, t:t + 1], hT[b][:, t * P:t * P + r], W2s[:, 0, KC * P:],
                                        start=True, stop=True)
                ins.then_inc(s_job, 1)

            pe.wait_ge(s_hTs, NB)
            pe.wait_ge(s_sgn, 2)
            for g in range(NG):
                u, r = g // EA_GROUPS, rows(g)
                if g % EA_GROUPS == 0:
                    pe.wait_ge(s_ea[u % EA_SLOTS], 16 * (u // EA_SLOTS + 1))
                if g >= 2:
                    pe.wait_ge(s_m, g - 1)
                for k in range(tiles(g)):
                    a = (g % EA_GROUPS) * GE + k * P
                    ins = pe.matmul(ps_m[g % 2][0:r, k * L:(k + 1) * L], ea_s[u % EA_SLOTS][:, a:a + r], W1c[:, :],
                                    start=True, stop=True)
                ins.then_inc(s_eam, 1)
                pe.wait_ge(s_hot, g + 1)
                for k in range(tiles(g)):
                    ins = pe.matmul(ps_cnt[0:NH, 0:P], hot_hi[0:r, g % 2, k, 0:NH], hot_lo[0:r, g % 2, k, :],
                                    start=(g == 0 and k == 0), stop=(g == NG - 1), skip_group_check=True)
                ins.then_inc(s_cnt, 1)
                if g >= 1:
                    stats(g - 1)
                if g == TURN:
                    pe.wait_ge(s_rng, 1)
                    pe.transpose(psum[0:2 * GC, 7, 0:P], rng[:, :], ident[:, :]).then_inc(s_rngT, 1)
                if g in job_of:
                    early_part(job_of[g])
            stats(NG - 1)
            pe.wait_ge(s_row, 1)
            pe.wait_ge(s_jobs, len(JOBS))
            for i, (v, h) in enumerate(((A, 0), (A, 1), (NEGT, 0), (NEGT, 1))):
                ins = pe.transpose(ps_col[:, i * P:(i + 1) * P], bn_row[:, v, h * P:(h + 1) * P], ident[:, :])
            ins.then_inc(s_col, 1)

            def window(nt, r, slot, sel_k, width, bank_ap, done):
                for k in range(nt):
                    for h in range(2):
                        ins = pe.matmul(bank_ap[:, h * width:(h + 1) * width],
                                        m_s[slot][0:r, k * L + h * P:k * L + (h + 1) * P], sel_k(k)[0:r, :],
                                        start=(k == 0 and h == 0), stop=(k == nt - 1), skip_group_check=True)
                ins.then_inc(done, 1)

            flag = pe.alloc_register("wide_pe")
            pe.wait_ge(s_flag, 1)
            pe.load(flag, wide_i[0:1, 0:1])
            with pe.If_eq(flag, 0):
                for g in range(NG):
                    pe.wait_ge(s_r, g + 1)
                    pe.wait_ge(s_sel, g + 1)
                    if g >= 3:
                        pe.wait_ge(s_add, g - 2)
                    window(tiles(g), rows(g), g % M_SLOTS, lambda k, g=g: sel[:, g % 4, k, :], WIN, ps_seg[g % 3], s_seg)
            with pe.Else():
                with pe.Fori(0, GF) as g:
                    with pe.Fori(0, NH) as w:
                        pe.wait_ge(fb_s, g * NH + w + 1)
                        window(GT, P, 0, lambda k: fb_sel[:, k, :], P, psum[:, 0, :], fb_pe)
                with pe.Fori(0, NH) as w:
                    pe.wait_ge(fb_s, w + (GF * NH + 1))
                    window(1, TAIL, 0, lambda k: fb_sel[:, k, :], P, psum[:, 0, :], fb_pe)

            for b in range(NB):
                n, c0 = block_nodes(b), b * BN_
                pe.wait_ge(s_n0, b + 1)
                if b >= 2:
                    pe.wait_ge(s_n1s, b - 1)
                bank = 4 * (b % 2)
                for t, a, r in tiles_of(b):
                    for h in range(2):
                        pe.matmul(psum[0:r, bank + KC, t:t + 1], plane[h][:, a:a + r], W2s[:, 1 + h, KC * P:],
                                  start=(h == 0), stop=(h == 1))
                for c in range(KC):
                    for h in range(2):
                        ins = pe.matmul(psum[:, bank + c, 0:n], W2s[:, 1 + h, c * P:(c + 1) * P],
                                        plane[h][:, c0:c0 + n], start=(h == 0), stop=(h == 1))
                ins.then_inc(s_n1, 1)
            pe.wait_ge(s_odd, 1)
            pe.matmul(psum[:, ODD_BANK, 0:2], ones[:, :], odd_sum[:, 0:2], start=True, stop=True).then_inc(s_oddm, 1)
            pe.wait_ge(s_n1s, NB)
            for b in range(NB):
                pe.wait_ge(s_r2, b + 1)
                if b >= 4:
                    pe.wait_ge(s_o, b - 3)
                for t, a, r in tiles_of(b):
                    o = psum[0:r, b % 4, t * P:(t + 1) * P]
                    for c in range(KC):
                        ins = pe.matmul(o, plane[c][:, a:a + r], W3s[:, c, :], start=(c == 0), stop=(c == KC - 1))
                ins.then_inc(s_n2, 1)


def kernel(x, src, dst, edge_attr_64, L0_gnn_u, L0_gnn_W1, L0_gnn_b1, L0_gnn_g1, L0_gnn_be1, L0_gnn_W2,
           L0_gnn_b2, L0_gnn_g2, L0_gnn_be2, L0_gnn_W3, L0_gnn_b3):
    import numpy as np
    import concourse.bacc as bacc
    from concourse.bass_utils import run_bass_kernel_spmd

    src, dst = np.asarray(src), np.asarray(dst)
    full = src.shape[0] // GE * GE

    def columns(v):
        return np.ascontiguousarray(v[:full].reshape(-1, P).T), np.ascontiguousarray(v[full:].reshape(-1, 1))

    src_main, src_tail = columns(src)
    dst_main, dst_tail = columns(dst)
    arrays = {
        "x": x, "src_main": src_main, "src_tail": src_tail, "dst_main": dst_main, "dst_tail": dst_tail, "dst": dst,
        "eaT": np.ascontiguousarray(np.asarray(edge_attr_64).T),
        "W1": L0_gnn_W1, "b1": L0_gnn_b1, "g1": L0_gnn_g1, "be1": L0_gnn_be1,
        "W2": L0_gnn_W2, "b2": L0_gnn_b2, "g2": L0_gnn_g2, "be2": L0_gnn_be2, "W3": L0_gnn_W3, "b3": L0_gnn_b3,
    }
    arrays = {k: np.ascontiguousarray(v) for k, v in arrays.items()}
    nc = bacc.Bacc("TRN2", target_bir_lowering=False, num_devices=1)
    aps = {k: nc.dram_tensor(f"in_{k}", v.shape, mybir.dt.from_np(v.dtype), kind="ExternalInput").ap()
           for k, v in arrays.items()}
    o = nc.dram_tensor("out", arrays["x"].shape, F32, kind="ExternalOutput").ap()
    build(nc, **aps, out=o)
    r = run_bass_kernel_spmd(nc, [{f"in_{k}": v for k, v in arrays.items()}], core_ids=[0])
    return r.results[0]["out"]
```
